# Optimizing a Trainium2 kernel written in Bass

```python
import numpy as np
import jax
import jax.numpy as jnp

def _softmax(x, axis=-1):
    return jax.nn.softmax(x, axis=axis)

def _gelu(x):
    return jax.nn.gelu(x, approximate=True)

def _silu(x):
    return jax.nn.silu(x)

def _sigmoid(x):
    return jax.nn.sigmoid(x)

def _layernorm(x, axis=-1, eps=1e-05):
    m = jnp.mean(x, axis=axis, keepdims=True)
    v = jnp.var(x, axis=axis, keepdims=True)
    return (x - m) / jnp.sqrt(v + eps)

def _scatter_add(tgt, idx, src, axis=0):
    return tgt.at[idx].add(src)

def _segment_sum(src, seg, n):
    return jax.ops.segment_sum(src, seg, n)
kernel_name = 'mk_adaln_d1_jaxref_r4_3c4aa2'

def setup_inputs(seed: int=0):
    np.random.seed(seed)
    _w = jnp.asarray

    def _L0_attn_setup():
        import jax, jax.numpy as jnp
        import numpy as np
        D_MODEL = 512
        GN_EPS = 1e-05
        key = jax.random.key(seed)
        ks = jax.random.split(key, 6)
        B, T, D = (4, 512, D_MODEL)
        s = 1.0 / np.sqrt(D)
        return {'x': jax.random.normal(ks[0], (B, T, D), dtype=jnp.float32), 'Wr': jax.random.normal(ks[1], (D, D), dtype=jnp.float32) * s, 'Wk': jax.random.normal(ks[2], (D, D), dtype=jnp.float32) * s, 'Wv': jax.random.normal(ks[3], (D, D), dtype=jnp.float32) * s, 'Wo': jax.random.normal(ks[4], (D, D), dtype=jnp.float32) * s, 'decay': jnp.ones((D,), dtype=jnp.float32) * 0.99, 'gn_weight': jnp.ones((D,), dtype=jnp.float32), 'gn_bias': jnp.zeros((D,), dtype=jnp.float32)}
    _L0_attn_in = _L0_attn_setup()

    def _L0_ffn_setup():
        import jax, jax.numpy as jnp
        import numpy as np
        B, S, D, H = (4, 512, 512, 2048)

        def fwht(x):
            orig_shape = x.shape
            n = orig_shape[-1]
            x = x.reshape(-1, n)
            h = 1
            while h < n:
                xb = x.reshape(-1, n // (2 * h), 2, h)
                a = xb[:, :, 0, :]
                b = xb[:, :, 1, :]
                x = jnp.stack([a + b, a - b], axis=2).reshape(-1, n)
                h *= 2
            scale = jnp.asarray(1.0 / np.sqrt(n), dtype=x.dtype)
            return (x * scale).reshape(orig_shape)
        key = jax.random.key(seed)
        kx, k1, k2, k3 = jax.random.split(key, 4)
        x = jax.random.normal(kx, (B, S, D), dtype=jnp.float32)
        W1 = jax.random.normal(k1, (H, D), dtype=jnp.float32) * (1.0 / np.sqrt(D))
        W2 = jax.random.normal(k2, (D, H), dtype=jnp.float32) * (1.0 / np.sqrt(H))
        W3 = jax.random.normal(k3, (H, D), dtype=jnp.float32) * (1.0 / np.sqrt(D))
        return {'x': x, 'W1': W1, 'W2': W2, 'W3': W3}
    _L0_ffn_in = _L0_ffn_setup()
    _L0_c = _w((lambda *s: np.random.randn(*s).astype(np.float32) * 0.05)(4, 512))
    _L0_wmod = _w((lambda *s: np.random.randn(*s).astype(np.float32) * 0.05)(512, 6 * 512) * 512 ** (-0.5))
    _d = {'L0_attn_x': _L0_attn_in['x'], 'L0_attn_Wr': _L0_attn_in['Wr'], 'L0_attn_Wk': _L0_attn_in['Wk'], 'L0_attn_Wv': _L0_attn_in['Wv'], 'L0_attn_Wo': _L0_attn_in['Wo'], 'L0_attn_decay': _L0_attn_in['decay'], 'L0_attn_gn_weight': _L0_attn_in['gn_weight'], 'L0_attn_gn_bias': _L0_attn_in['gn_bias'], 'L0_ffn_W1': _L0_ffn_in['W1'], 'L0_ffn_W2': _L0_ffn_in['W2'], 'L0_ffn_W3': _L0_ffn_in['W3'], 'L0_c': _L0_c, 'L0_wmod': _L0_wmod}
    _x0 = _d['L0_attn_x']
    _d['L0_attn_x'] = jax.random.normal(jax.random.fold_in(jax.random.key(seed), 1), (4, 2048, 512), dtype=_x0.dtype)
    del _x0
    return _d

def reference(L0_attn_x, L0_attn_Wr, L0_attn_Wk, L0_attn_Wv, L0_attn_Wo, L0_attn_decay, L0_attn_gn_weight, L0_attn_gn_bias, L0_ffn_W1, L0_ffn_W2, L0_ffn_W3, L0_c, L0_wmod):

    def _L0_attn_ref(x, Wr, Wk, Wv, Wo, decay, gn_weight, gn_bias):
        import jax, jax.numpy as jnp
        import numpy as np
        D_MODEL = 512
        GN_EPS = 1e-05
        B, T, D = x.shape
        r = jax.nn.sigmoid(jnp.einsum('btd,ed->bte', x, Wr))
        k = jnp.einsum('btd,ed->bte', x, Wk)
        v = jnp.einsum('btd,ed->bte', x, Wv)
        d = jax.nn.sigmoid(decay)
        log_decay = jnp.log(jnp.clip(d, 1e-07, None))
        pos = jnp.arange(T, dtype=x.dtype)
        scale = jnp.exp(pos[:, None] * log_decay[None, :])
        scaled = k * v / jnp.clip(scale, 1e-10, None)[None]
        state = jnp.cumsum(scaled, axis=1) * scale[None]
        out = r * state
        mean = jnp.mean(out, axis=(1, 2), keepdims=True)
        var = jnp.mean(jnp.square(out - mean), axis=(1, 2), keepdims=True)
        normed = (out - mean) * jax.lax.rsqrt(var + GN_EPS)
        normed = normed * gn_weight + gn_bias
        return jnp.einsum('btd,ed->bte', normed, Wo)

    def _L0_ffn_ref(x, W1, W2, W3):
        import jax, jax.numpy as jnp
        import numpy as np
        B, S, D, H = (4, 512, 512, 2048)

        def fwht(x):
            orig_shape = x.shape
            n = orig_shape[-1]
            x = x.reshape(-1, n)
            h = 1
            while h < n:
                xb = x.reshape(-1, n // (2 * h), 2, h)
                a = xb[:, :, 0, :]
                b = xb[:, :, 1, :]
                x = jnp.stack([a + b, a - b], axis=2).reshape(-1, n)
                h *= 2
            scale = jnp.asarray(1.0 / np.sqrt(n), dtype=x.dtype)
            return (x * scale).reshape(orig_shape)
        up_gate = jnp.einsum('bsd,hd->bsh', x, W1)
        up_lin = jnp.einsum('bsd,hd->bsh', x, W3)
        hidden = jax.nn.silu(up_gate) * up_lin
        hidden = fwht(hidden)
        out = jnp.einsum('bsh,dh->bsd', hidden, W2)
        return out
    x = L0_attn_x
    mod = (_silu(L0_c) @ L0_wmod).reshape(L0_c.shape[0], 6, 1, -1)
    sa, ca, ga, sb, cb, gb = (mod[:, 0], mod[:, 1], mod[:, 2], mod[:, 3], mod[:, 4], mod[:, 5])
    ga = (2 * (ga >= 0) - 1) * jnp.maximum(jnp.abs(ga), 0.25)
    gb = (2 * (gb >= 0) - 1) * jnp.maximum(jnp.abs(gb), 0.25)
    h = _layernorm(x, axis=-1) * (1 + ca) + sa
    x = x + ga * _L0_attn_ref(h, L0_attn_Wr, L0_attn_Wk, L0_attn_Wv, L0_attn_Wo, L0_attn_decay, L0_attn_gn_weight, L0_attn_gn_bias)
    h = _layernorm(x, axis=-1) * (1 + cb) + sb
    x = x + gb * _L0_ffn_ref(h, L0_ffn_W1, L0_ffn_W2, L0_ffn_W3)
    return x

_drawn_inputs = setup_inputs


def setup_inputs(seed=0):
    import zlib

    import numpy as np

    out = dict(_drawn_inputs(seed))
    spreads = {'L0_attn_decay': (0.9900000095367432, 0.2),
     'L0_attn_gn_weight': (1.0, 0.2),
     'L0_attn_gn_bias': (0.0, 0.349)}
    factors = {}
    for name, (base, spread) in spreads.items():
        noise = np.random.default_rng([zlib.crc32(name.encode()), seed]).standard_normal(out[name].shape)
        drawn = base * np.exp(spread * noise) if base else spread * noise
        out[name] = jnp.asarray(drawn.astype(out[name].dtype))
    for name, factor in factors.items():
        out[name] = (out[name] * factor).astype(out[name].dtype)
    return out
```

```python
from contextlib import ExitStack

import numpy as np

import concourse.bass as bass
from concourse import mybir

ALU = mybir.AluOpType
ACT = mybir.ActivationFunctionType
AX = mybir.AxisListType
F32 = mybir.dt.float32
F16 = mybir.dt.float16
I32 = mybir.dt.int32
RMAX = bass.bass_isa.ReduceOp.max
RADD = bass.bass_isa.ReduceOp.add

P = 128
NB, SEQ, D, H = 4, 2048, 512, 2048
T = 512
TPB = SEQ // T
NT = NB * TPB
KC = D // P
TC = T // P
HC = H // P
EPS = 1e-5
EXPONENT = 0x7F800000
TOP = 2.0 ** 14
SA, CA, GA, SB, CB, GB = range(6)
S_ATT, S_H1, S_H2, S_N, S_FFN, S_W2, S_HID = range(7)
SLOTS = [*range(10), "t0", 10, 11, "t1", *range(12, HC)]


def waits(eng, sem, count):
    if not isinstance(count, int) or count > 0:
        eng.wait_ge(sem, count)


def adaln_block_kernel(nc, x, w_att, w13, w2t, c_t, w_mod, columns, identity, hadamard, out):
    with ExitStack() as ctx:
        def sem(name):
            return ctx.enter_context(nc.semaphore(name))

        arena = ctx.enter_context(nc.sbuf_tensor("arena", [P, 206 * 256], F32))

        def place(kb, shape, dt=F32):
            n = int(np.prod(shape[1:]))
            words = n if dt == F32 else n // 2
            at = int(kb * 256)
            view = arena[:, at:at + words]
            if dt != F32:
                view = view.bitcast(dt)
            if len(shape) == 3:
                view = view.rearrange("p (a b) -> p a b", a=shape[1])
            if len(shape) == 4:
                view = view.rearrange("p (a b c) -> p a b c", a=shape[1], b=shape[2])
            return view

        w_rkv = place(0, [P, 3 * KC, 2 * D], F16)
        h1t = [place(24 + 8 * i, [P, KC, 2 * T], F16) for i in range(2)]
        xa = place(40, [P, TC, D])
        decay_pow = place(48, [P, KC, T])
        state = place(56, [P, KC, T])
        r_buf = place(64, [P, KC, T])
        kv_buf = place(72, [P, 2, T])
        w_buf = place(76, [P, 2, T])
        h_tmp = place(80, [P, 2, T])
        stage_a = place(86, [P, 2048])
        stage_b = place(94, [P, 2048])
        stage_h = place(102, [P, 2, 2048], F16)
        w_o = place(110, [P, KC, 2 * D], F16)
        slots = place(118, [P, TPB * KC, T])
        n_t = place(150, [P, KC, 2 * T], F16)
        xr = [place(158 + 8 * i, [P, TC, D]) for i in range(2)]
        n_tmp = place(174, [P, 2, T])
        o_tmp = place(178, [P, 2, D])
        gate_a = place(182, [P, NB, D])
        small = place(190, [P, 512])
        w13_sb = place(0, [P, 2 * KC, 2 * H], F16)
        w2_sb = place(64, [P, HC, 2 * D], F16)
        xh = place(96, [P, TC, D])
        hid32 = place(104, [P, 2, T])
        h2t = [place(192, [P, KC, 2 * T], F16), place(118, [P, KC, 2 * T], F16)]
        x1 = [place(126, [P, TC, D]), place(134, [P, TC, D])]
        hid16 = place(142, [P, 2, 2 * T], F16)
        h2_tmp = place(146, [P, 2, T])
        f_tmp = place(200, [P, 2, D])
        gate_b = place(182, [P, NB, D])
        wmod_sb = place(118, [P, KC, 4 * D])
        mod_rows = place(192, [P, 6 * D])
        row_tmp = place(178, [P, 2, D])
        watt_stage = [xr[0], xr[1], stage_a.rearrange("p (a b) -> p a b", a=KC),
                      stage_b.rearrange("p (a b) -> p a b", a=KC)]
        ident = place(204, [P, P])
        had = place(204.5, [P, P])

        used = [0]

        def few(n):
            used[0] += n
            assert used[0] <= 512
            return small[:, used[0] - n:used[0]]

        cols = few(3 * KC)
        ct, silu_c = few(KC * NB), few(KC * NB)
        mod_t = [few(KC * NB) for _ in range(4)]
        ln_a, ln_b = few(2 * NB * KC), few(2 * NB * KC)
        peaks, block_peaks = few(8), few(12)
        peak, later_peak, later_own = few(8), few(2), few(2)
        bound, pow2, recip2, scale, unscale = few(8), few(8), few(8), few(8), few(8)
        bound_tmp, w2_scale = few(4), few(1)
        un_qkv, un_o, un_gate, un_up, un_w2 = few(1), few(1), few(1), few(1), few(1)
        dec, d_tile = few(KC), few(KC)
        fac = few(TPB * KC)
        zero_col = few(1)
        stats, mv = few(TC * 6), few(TC * 2)
        var_eps, rstd, neg_half = few(TC), few(TC), few(TC)
        gn_stats, gn_mv = few(TPB * KC * 6), few(2)
        gn_all, gn_mean, gn_dev, gn_dev2, gn_sum, gn_sum_all = few(1), few(1), few(1), few(1), few(1), few(1)
        gn_var, gn_rstd = few(1), few(1)
        gn_a, gn_b, gn_mw = few(KC), few(KC), few(KC)
        gn_w_scaled, gn_b_scaled = few(KC), few(KC)

        def coef(tile, norm, b, c):
            return tile[:, bass.ds(norm * NB * KC + b * KC + c, 1)]

        ps = [ctx.enter_context(nc.psum_tensor(f"bank{i}", [P, 512], F32)) for i in range(8)]

        def bank_rkv(c, o):
            return 4 + (3 * c + o) % 4

        def bank_ffn(k):
            return 4 + 2 * (SLOTS.index(k) % 2)

        gates_dram = nc.dram_tensor("gates_scratch", [2, NB * D], F32).ap()
        x1_dram = nc.dram_tensor("x1_scratch", [NT, P, TC * D], F32).ap()
        w13_dram = nc.dram_tensor("w13_scratch", [2, KC, P, 2 * H], F16).ap()
        w2_dram = nc.dram_tensor("w2_scratch", [P, HC, 2, D], F16).ap()

        x_tiles = x.rearrange("(n c p) d -> n p c d", c=TC, p=P)
        out_tiles = out.rearrange("(n c p) d -> n p c d", c=TC, p=P)
        w_att_v = w_att.rearrange("m (k p) e -> m p k e", p=P)
        w13_v = w13.rearrange("m (k p) h -> m k p h", p=P)
        w2_rows = w2t.rearrange("(g j p) d -> g p j d", j=KC, p=P)
        w2_cols = w2t.rearrange("(j p) (g d) -> g p j d", p=P, d=P)
        w_mod_v = w_mod.rearrange("(k p) n -> p k n", p=P)

        passed = sem("passed")
        consts_in = sem("consts_in")
        watt_in = [sem(f"watt_in{i}") for i in range(4)]
        wmod_in = [sem(f"wmod_in{i}") for i in range(3)]
        silu_done = sem("silu_done")
        mod_ready = sem("mod_ready")
        mod_copied = sem("mod_copied")
        modt_ready = sem("modt_ready")
        modt_copied = sem("modt_copied")
        gates_done = sem("gates_done")
        gates_out = sem("gates_out")
        gate_a_in = sem("gate_a_in")
        gate_b_in = sem("gate_b_in")
        dve_step = sem("dve_step")
        peaks_done = sem("peaks_done")
        peak_all = sem("peak_all")
        scales_done = sem("scales_done")
        block_peak = sem("block_peak")
        later_all = sem("later_all")
        later_scales = sem("later_scales")
        wscaled = sem("wscaled")
        whi = sem("whi")
        wsplit = sem("wsplit")
        xa_in = sem("xa_in")
        ln_stat = sem("ln_stat")
        ln_var = sem("ln_var")
        ln_rstd = sem("ln_rstd")
        ln_done = sem("ln_done")
        t1_ready = sem("t1_ready")
        h1_read = sem("h1_read")
        h1_hi = sem("h1_hi")
        h1_done = sem("h1_done")
        v_ready = sem("v_ready")
        k_ready = sem("k_ready")
        r_ready = sem("r_ready")
        v_read = sem("v_read")
        r_read = sem("r_read")
        kv_done = sem("kv_done")
        w_done = sem("w_done")
        wkv_done = sem("wkv_done")
        state_done = sem("state_done")
        out_done = sem("out_done")
        out_stat = sem("out_stat")
        gn_mv_done = sem("gn_mv_done")
        gn_step = sem("gn_step")
        gn_done = sem("gn_done")
        n_read = sem("n_read")
        n_hi = sem("n_hi")
        n_done = sem("n_done")
        wo_ready = sem("wo_ready")
        wo_read = sem("wo_read")
        x1_done = sem("x1_done")
        xr_in = [sem(f"xr_in{i}") for i in range(2)]
        x1_out = [sem(f"x1_out{i}") for i in range(2)]
        max_in = [sem(f"max_in{i}") for i in range(2)]
        prep_in = sem("prep_in")
        prep_scaled = sem("prep_scaled")
        prep_hi = sem("prep_hi")
        prep_lo = sem("prep_lo")
        prep_out = sem("prep_out")
        prep2_in = sem("prep2_in")
        butterfly = sem("butterfly")
        had_ready = sem("had_ready")
        had_read = sem("had_read")
        prep2_hi = sem("prep2_hi")
        prep2_lo = sem("prep2_lo")
        prep2_out = sem("prep2_out")
        w13_in = sem("w13_in")
        w2_in = sem("w2_in")
        x1_in = [sem(f"x1_in{i}") for i in range(2)]
        ln2_stat = sem("ln2_stat")
        ln2_var = sem("ln2_var")
        ln2_rstd = sem("ln2_rstd")
        ln2_done = sem("ln2_done")
        t2_ready = sem("t2_ready")
        h2_read = sem("h2_read")
        h2_hi = sem("h2_hi")
        h2_done = sem("h2_done")
        gate_ready = sem("gate_ready")
        up_ready = sem("up_ready")
        sig_done = sem("sig_done")
        gated = sem("gated")
        hid_done = sem("hid_done")
        hid_hi = sem("hid_hi")
        hid_split = sem("hid_split")
        w2_used = sem("w2_used")
        acc_ready = sem("acc_ready")
        acc_read = sem("acc_read")
        y_done = sem("y_done")
        y_out = [sem(f"y_out{i}") for i in range(2)]

        HEAD_START = [(n_read, KC * TPB), (n_done, KC * TPB), (wo_ready, TC * TPB), (wo_read, TC * TPB),
                      (x1_done, TC * TPB), (prep_lo, TPB), (prep_out, 16 * TPB),
                      (gated, HC), (hid_done, HC), (hid_split, HC), (w2_used, HC - 1),
                      (acc_ready, TC), (acc_read, TC), (y_done, TC)]

        block = ctx.enter_context(nc.Block())

        @block.sync
        def _(sp):
            sp.dma_start(cols, columns).then_inc(consts_in, 16)
            sp.dma_start(ct, c_t).then_inc(consts_in, 16)
            sp.dma_start(ident, identity).then_inc(consts_in, 16)
            sp.dma_start(had, hadamard).then_inc(consts_in, 16)
            sp.dma_start(wmod_sb[:, :, 0:2 * D], w_mod_v[:, :, 0:2 * D]).then_inc(wmod_in[0], 16)
            sp.dma_start(xa, x_tiles[0]).then_inc(xa_in, 16)
            for i in range(4):
                sp.dma_start(watt_stage[i], w_att_v[i]).then_inc(watt_in[i], 16)
            sp.dma_start(wmod_sb[:, :, 2 * D:4 * D], w_mod_v[:, :, 2 * D:4 * D]).then_inc(wmod_in[1], 16)
            sp.wait_ge(mod_ready, 2)
            sp.dma_start(wmod_sb[:, :, 0:2 * D], w_mod_v[:, :, 4 * D:6 * D]).then_inc(wmod_in[2], 16)
            sp.wait_ge(gates_done, 2)
            for i, v in enumerate((GA, GB)):
                sp.dma_start(gates_dram[i].rearrange("(b d) -> b d", b=NB), mod_rows[0:NB, v * D:(v + 1) * D]
                             ).then_inc(gates_out, 16)
            sp.wait_ge(gates_out, 32)
            sp.dma_start(gate_a.rearrange("p b d -> p (b d)"), gates_dram[0:1].to_broadcast([P, NB * D])
                         ).then_inc(gate_a_in, 16)
            sp.wait_ge(t1_ready, KC)
            sp.dma_start(xa, x_tiles[1]).then_inc(xa_in, 16)

            def load_block(i):
                if i < 2:
                    sp.wait_ge(wsplit, 4)
                else:
                    sp.wait_ge(block_peak, i - 1)
                stage = (stage_a, stage_b)[i % 2]
                if i < 2 * KC:
                    sp.dma_start(stage, w13_v[i // KC, i % KC]).then_inc(max_in[i % 2], 16)
                else:
                    sp.dma_start(stage.rearrange("p (a b) -> p a b", a=KC), w2_rows[i - 2 * KC]).then_inc(max_in[i % 2], 16)

            def phase1(b, wo, prep, last=False):
                for t in range(TPB):
                    n = b * TPB + t
                    if prep == "max":
                        load_block(3 * t)
                        load_block(3 * t + 1)
                    if prep == "w13":
                        sp.wait_ge(block_peak, 3 * KC)
                        sp.wait_ge(prep_lo, n)
                        sp.dma_start(stage_a, w13_v[b - 1, t]).then_inc(prep_in, 16)
                    if prep != "none" and not (last and t >= TPB - 2):
                        sp.wait_ge(t1_ready, KC * (n + 2))
                        sp.dma_start(xa, x_tiles[n + 2]).then_inc(xa_in, 16)
                    if prep == "max":
                        load_block(3 * t + 2)
                        if t >= 2:
                            sp.dma_start(xr[t - 2], x_tiles[t - 2]).then_inc(xr_in[t - 2], 16)
                    if prep == "w2":
                        sp.wait_ge(prep_lo, 3 * TPB)
                        waits(sp, had_ready, 4 * t)
                        sp.dma_start(stage_a.rearrange("p (a b) -> p a b", a=HC), w2_cols[t]).then_inc(prep2_in, 16)
                    if wo:
                        sp.wait_ge(x1_done, TC * (n + 1))
                        sp.dma_start(x1_dram[n - TPB], xr[t % 2].rearrange("p a b -> p (a b)")).then_inc(x1_out[t % 2], 16)
                        sp.wait_ge(x1_out[t % 2], 32 * (b - 1) + 16 * (t // 2 + 1))
                        if prep != "none" or t < 2:
                            sp.dma_start(xr[t % 2], x_tiles[n - 2]).then_inc(xr_in[t % 2], 16)
                    if prep == "w13":
                        sp.wait_ge(prep_lo, n + 1)
                        sp.dma_start(w13_dram[b - 1, t], stage_h.rearrange("p a b -> p (a b)")).then_inc(prep_out, 16)
                    if prep == "w2" and t > 0:
                        store_w2(t - 1)
                    if prep == "none" and t == 0:
                        store_w2(TPB - 1)
                        sp.wait_ge(out_done, KC * NT)
                        sp.wait_ge(out_stat, KC * NT)
                        sp.wait_ge(prep2_out, 32 * TPB)
                        sp.wait_ge(prep_out, 16 * 3 * TPB)
                        for i in range(2 * KC):
                            sp.dma_start(w13_sb[:, i, :], w13_dram[i // KC, i % KC]).then_inc(w13_in, 16)
                        sp.dma_start(w2_sb.rearrange("p a b -> p (a b)"), w2_dram.rearrange("p a b c -> p (a b c)")
                                     ).then_inc(w2_in, 16)
                    if prep == "none" and t in (1, 2):
                        sp.wait_ge(n_read, KC * (n + 1))
                        sp.dma_start(x1[t - 1].rearrange("p a b -> p (a b)"), x1_dram[t - 1]).then_inc(x1_in[t - 1], 16)

            def store_w2(t):
                sp.wait_ge(prep2_lo, t + 1)
                for i in range(2):
                    sp.dma_start(w2_dram[:, :, i, P * t:P * (t + 1)],
                                 stage_h[:, i, :].rearrange("p (a b) -> p a b", a=HC)).then_inc(prep2_out, 16)

            phase1(0, False, "max")
            with sp.Fori(1, 3) as b:
                phase1(b, True, "w13")
            phase1(3, True, "w2", last=True)
            phase1(4, True, "none")

            sp.dma_start(gate_b.rearrange("p b d -> p (b d)"), gates_dram[1:2].to_broadcast([P, NB * D])
                         ).then_inc(gate_b_in, 16)

            def phase2(s, i, more):
                sp.wait_ge(y_done, TC * (s + 2))
                sp.dma_start(out_tiles[s], x1[i]).then_inc(y_out[i], 16)
                if more:
                    sp.wait_ge(y_out[i], (s - i) * 8 + 16)
                    sp.dma_start(x1[i].rearrange("p a b -> p (a b)"), x1_dram[s + 2]).then_inc(x1_in[i], 16)

            with sp.Fori(0, NT // 2 - 1) as pair:
                phase2(pair * 2, 0, True)
                phase2(pair * 2 + 1, 1, True)
            phase2(NT - 2, 0, False)
            phase2(NT - 1, 1, False)
            for i in range(2):
                sp.wait_ge(y_out[i], 16 * NT // 2)

        @block.gpsimd
        def _(pool):
            for s, count in HEAD_START:
                nc.gpsimd.sem_inc(s, count)
            nc.gpsimd.memset(neg_half, -0.5).then_inc(gn_step, 1)
            pool.wait_ge(gn_step, 1)
            pool.wait_ge(ln_var, 1)
            nc.gpsimd.tensor_tensor(rstd, var_eps, neg_half, ALU.pow).then_inc(ln_rstd, 1)
            pool.wait_ge(peaks_done, 4)
            nc.gpsimd.partition_all_reduce(peak, peaks, P, RMAX).then_inc(peak_all, 1)
            for i in range(4):
                w = w_rkv[:, KC * i:KC * (i + 1), :] if i < 3 else w_o
                pool.wait_ge(whi, i + 1)
                nc.gpsimd.tensor_tensor(w[:, :, D:], watt_stage[i], w[:, :, 0:D], ALU.subtract).then_inc(wsplit, 1)

            def batch_norm(b):
                def after(i):
                    pool.wait_ge(gn_step, 10 * b + 1 + i)
                    pool.sem_inc(passed, 1)

                pool.wait_ge(gn_mv_done, b + 1)
                pool.sem_inc(passed, 1)
                nc.gpsimd.partition_all_reduce(gn_all, gn_mv[:, 0:1], P, RADD).then_inc(gn_step, 1)
                after(1)
                nc.gpsimd.tensor_scalar(gn_mean, gn_all, 1.0 / P, None, ALU.mult).then_inc(gn_step, 1)
                after(2)
                nc.gpsimd.tensor_tensor(gn_dev, gn_mv[:, 0:1], gn_mean, ALU.subtract).then_inc(gn_step, 1)
                after(3)
                nc.gpsimd.tensor_tensor(gn_dev2, gn_dev, gn_dev, ALU.mult).then_inc(gn_step, 1)
                after(4)
                nc.gpsimd.tensor_tensor(gn_sum, gn_dev2, gn_mv[:, 1:2], ALU.add).then_inc(gn_step, 1)
                after(5)
                nc.gpsimd.partition_all_reduce(gn_sum_all, gn_sum, P, RADD).then_inc(gn_step, 1)
                after(6)
                nc.gpsimd.tensor_scalar(gn_var, gn_sum_all, 1.0 / P, EPS, ALU.mult, ALU.add).then_inc(gn_step, 1)
                after(7)
                nc.gpsimd.tensor_tensor(gn_rstd, gn_var, neg_half[:, 0:1], ALU.pow).then_inc(gn_step, 1)
                after(8)
                pool.wait_ge(n_read, KC * TPB * (b + 1))
                pool.sem_inc(passed, 1)
                nc.gpsimd.tensor_scalar(gn_a, gn_w_scaled, gn_rstd, None, ALU.mult).then_inc(gn_step, 1)
                after(9)
                nc.gpsimd.tensor_scalar(gn_mw, gn_a, gn_mean, None, ALU.mult).then_inc(gn_step, 1)
                after(10)
                nc.gpsimd.tensor_tensor(gn_b, gn_b_scaled, gn_mw, ALU.subtract).then_inc(gn_done, 1)

            def low_w2(t):
                pool.wait_ge(prep2_hi, t + 1)
                if t == 0:
                    pool.wait_ge(prep_out, 16 * 3 * TPB)
                else:
                    pool.wait_ge(prep2_out, 32 * t)
                nc.gpsimd.tensor_tensor(stage_h[:, 1, :], stage_b, stage_h[:, 0, :], ALU.subtract).then_inc(prep2_lo, 1)

            def phase1(b, qkv, wo, prep, last=False):
                for t in range(TPB):
                    n = b * TPB + t
                    if qkv and not (last and t == TPB - 1):
                        pool.wait_ge(ln_var, n + 2)
                        nc.gpsimd.tensor_tensor(rstd, var_eps, neg_half, ALU.pow).then_inc(ln_rstd, 1)
                    if qkv:
                        for c in range(KC):
                            pool.wait_ge(r_read, KC * n + c + 1)
                            pool.wait_ge(state_done, KC * n + c + 1)
                            pool.wait_ge(n_read, KC * n + c + 1)
                            if wo:
                                pool.wait_ge(out_stat, KC * (n - TPB) + c + 1)
                            nc.gpsimd.tensor_tensor(slots[:, KC * t + c, :], state[:, c, :], r_buf[:, c, :], ALU.mult
                                                    ).then_inc(out_done, 1)
                        if t == TPB - 1:
                            batch_norm(b)
                    if prep == "none" and t == 0:
                        low_w2(TPB - 1)
                    if prep == "none" and t == 2:
                        pool.wait_ge(ln2_var, 1)
                        nc.gpsimd.tensor_tensor(rstd, var_eps, neg_half, ALU.pow).then_inc(ln2_rstd, 1)
                    if wo:
                        for c in range(TC):
                            pool.wait_ge(wo_read, TC * n + c + 1)
                            pool.wait_ge(xr_in[t % 2], 32 * (b - 1) + 16 * (t // 2 + 1))
                            nc.gpsimd.tensor_tensor(xr[t % 2][:, c, :], xr[t % 2][:, c, :], o_tmp[:, c % 2, :], ALU.add
                                                    ).then_inc(x1_done, 1)
                    if prep == "max" and t == TPB - 1:
                        pool.wait_ge(block_peak, 3 * KC + 2)
                        nc.gpsimd.partition_all_reduce(later_peak, later_own, P, RMAX).then_inc(later_all, 1)
                    if prep == "w13":
                        pool.wait_ge(prep_hi, n - TPB + 1)
                        pool.wait_ge(prep_out, 16 * n)
                        nc.gpsimd.tensor_tensor(stage_h[:, 1, :], stage_a, stage_h[:, 0, :], ALU.subtract).then_inc(prep_lo, 1)
                    if prep == "w2":
                        if t > 0:
                            low_w2(t - 1)
                        pool.wait_ge(prep2_in, 16 * (t + 1))
                        for i in range(4):
                            if i > 0:
                                pool.wait_ge(butterfly, 8 * t + 2 * i)
                            elif t > 0:
                                pool.wait_ge(prep2_lo, t)
                            src, dst = (stage_a, stage_b) if i % 2 == 0 else (stage_b, stage_a)
                            src = src.rearrange("p (a two h) -> p a two h", two=2, h=P << i)
                            dst = dst.rearrange("p (a two h) -> p a two h", two=2, h=P << i)
                            nc.gpsimd.tensor_tensor(dst[:, :, 0, :], src[:, :, 0, :], src[:, :, 1, :], ALU.add
                                                    ).then_inc(butterfly, 1)
                            nc.gpsimd.tensor_tensor(dst[:, :, 1, :], src[:, :, 0, :], src[:, :, 1, :], ALU.subtract
                                                    ).then_inc(butterfly, 1)

            phase1(0, True, False, "max")
            with pool.Fori(1, 3) as b:
                phase1(b, True, True, "w13")
            phase1(3, True, True, "w2", last=True)
            phase1(4, False, True, "none")

            def phase2(s, i, more):
                if more:
                    pool.wait_ge(ln2_var, s + 2)
                    nc.gpsimd.tensor_tensor(rstd, var_eps, neg_half, ALU.pow).then_inc(ln2_rstd, 1)
                for c in range(TC):
                    pool.wait_ge(acc_read, TC * (s + 1) + c + 1)
                    nc.gpsimd.tensor_tensor(x1[i][:, c, :], x1[i][:, c, :], f_tmp[:, c % 2, :], ALU.add
                                            ).then_inc(y_done, 1)

            with pool.Fori(0, NT // 2 - 1) as pair:
                phase2(pair * 2, 0, True)
                phase2(pair * 2 + 1, 1, True)
            phase2(NT - 2, 0, True)
            phase2(NT - 1, 1, False)

        @block.scalar
        def _(act):
            def copy(dst, src, scale=1.0):
                return nc.scalar.activation(dst, src, ACT.Copy, scale=scale)

            def modulate1(b, t, n):
                for c in range(KC):
                    act.wait_ge(t1_ready, KC * n + c + 1)
                    if isinstance(n, int) and KC * n + c < 2:
                        pass
                    else:
                        act.wait_ge(h1_done, KC * n + c - 1)
                    act.sem_inc(passed, 1)
                    nc.scalar.activation(h_tmp[:, c % 2, :], ps[c][:, :], ACT.Identity, scale=coef(ln_a, 0, b, c),
                                         bias=coef(ln_b, 0, b, c)).then_inc(h1_read, 1)

            def modulate2(b, s, chunks, banks):
                for c, bank in zip(chunks, banks):
                    act.wait_ge(t2_ready, KC * s + c + 1)
                    if isinstance(s, int) and KC * s + c < 2:
                        pass
                    else:
                        act.wait_ge(h2_done, KC * s + c - 1)
                    act.sem_inc(passed, 1)
                    nc.scalar.activation(h2_tmp[:, c % 2, :], ps[bank][:, :], ACT.Identity, scale=coef(ln_a, 1, b, c),
                                         bias=coef(ln_b, 1, b, c)).then_inc(h2_read, 1)

            act.wait_ge(consts_in, 64)
            nc.scalar.activation(silu_c, ct, ACT.Sigmoid).then_inc(silu_done, 1)
            nc.scalar.activation(dec, cols[:, 0:KC], ACT.Sigmoid).then_inc(silu_done, 1)
            for v in (SA, CA, GA, SB, CB, GB):
                act.wait_ge(mod_ready, v + 1)
                copy(mod_rows[0:NB, v * D:(v + 1) * D], ps[v % 4][0:NB, :]).then_inc(mod_copied, 1)
            act.wait_ge(scales_done, 4)
            for i in range(4):
                w = w_rkv[:, KC * i:KC * (i + 1), :] if i < 3 else w_o
                copy(watt_stage[i], watt_stage[i], scale[:, S_ATT:S_ATT + 1]).then_inc(wscaled, 1)
                act.wait_ge(wscaled, i + 1)
                copy(w[:, :, 0:D], watt_stage[i]).then_inc(whi, 1)
            modulate1(0, 0, 0)

            def split_w2(t):
                for i in range(4):
                    act.wait_ge(had_ready, 4 * t + i + 1)
                    copy(stage_b[:, T * i:T * (i + 1)], ps[i][:, :], w2_scale).then_inc(had_read, 1)
                act.wait_ge(had_read, 4 * t + 4)
                if t == 0:
                    act.wait_ge(prep_out, 16 * 3 * TPB)
                else:
                    act.wait_ge(prep2_out, 32 * t)
                copy(stage_h[:, 0, :], stage_b).then_inc(prep2_hi, 1)

            def phase1(b, qkv, wo, prep, last=False):
                for t in range(TPB):
                    n = b * TPB + t
                    if wo:
                        for c in range(KC):
                            act.wait_ge(gn_done, b)
                            act.wait_ge(n_done, KC * n + c - 1)
                            nc.scalar.activation(n_tmp[:, c % 2, :], slots[:, KC * t + c, :], ACT.Identity,
                                                 scale=gn_a[:, c:c + 1], bias=gn_b[:, c:c + 1]).then_inc(n_read, 1)
                    if prep == "none" and t == 0:
                        split_w2(TPB - 1)
                    if prep == "none" and t == 3:
                        act.wait_ge(n_read, KC * (NT + TPB))
                        modulate2(0, 0, range(KC), range(4, 8))
                    if qkv:
                        for c in range(KC):
                            g = KC * n + c
                            act.wait_ge(v_ready, g + 1)
                            if not (isinstance(g, int) and g < 2):
                                act.wait_ge(state_done, g - 1)
                            copy(kv_buf[:, c % 2, :], ps[bank_rkv(c, 0)][:, :], un_qkv).then_inc(v_read, 1)
                            act.wait_ge(r_ready, g + 1)
                            if not (isinstance(g, int) and g < 4):
                                act.wait_ge(out_done, g - 3)
                            nc.scalar.activation(r_buf[:, c, :], ps[bank_rkv(c, 2)][:, :], ACT.Sigmoid, scale=un_qkv
                                                 ).then_inc(r_read, 1)
                            if c == 1 and not (last and t == TPB - 1):
                                modulate1(b + (t + 1) // TPB, (t + 1) % TPB, n + 1)
                            if c == 2 and prep == "w2" and t > 0:
                                split_w2(t - 1)
                    if prep == "w13":
                        act.wait_ge(later_scales, 1)
                        act.wait_ge(prep_in, 16 * (n - TPB + 1))
                        copy(stage_a, stage_a, scale[:, S_FFN:S_FFN + 1]).then_inc(prep_scaled, 1)
                        act.wait_ge(prep_scaled, n - TPB + 1)
                        act.wait_ge(prep_out, 16 * n)
                        copy(stage_h[:, 0, :], stage_a).then_inc(prep_hi, 1)

            phase1(0, True, False, "max")
            with act.Fori(1, 3) as b:
                phase1(b, True, True, "w13")
            phase1(3, True, True, "w2", last=True)
            phase1(4, False, True, "none")

            def phase2(s, i, more, b_next):
                for k in SLOTS:
                    if k == "t0" and more:
                        modulate2(b_next, s + 1, (0, 1), (bank_ffn(k), bank_ffn(k) + 1))
                    if k == "t1" and more:
                        modulate2(b_next, s + 1, (2, 3), (bank_ffn(k), bank_ffn(k) + 1))
                    if isinstance(k, str):
                        continue
                    g = s * HC + k
                    act.wait_ge(gate_ready, g + 1)
                    act.wait_ge(hid_split, g + HC - 1)
                    nc.scalar.activation(hid32[:, k % 2, :], ps[bank_ffn(k)][:, :], ACT.Sigmoid, scale=un_gate
                                         ).then_inc(sig_done, 1)
                    act.wait_ge(hid_done, g + HC + 1)
                    if k == 1:
                        act.wait_ge(acc_ready, TC * (s + 1))
                    else:
                        act.wait_ge(w2_used, (s + 1) * (HC - 1) + max(k - 1, 0))
                    copy(hid16[:, k % 2, 0:T], hid32[:, k % 2, :]).then_inc(hid_hi, 1)

            with act.Fori(0, NT // 2 - 1) as pair:
                phase2(pair * 2, 0, True, pair * 2 // TPB)
                phase2(pair * 2 + 1, 1, True, (pair * 2 + 2) // TPB)
            phase2(NT - 2, 0, True, NB - 1)
            phase2(NT - 1, 1, False, None)

        @block.vector
        def _(dve):
            steps = [0]

            def done(instruction):
                steps[0] += 1
                instruction.then_inc(dve_step, 1)
                dve.wait_ge(dve_step, steps[0])

            def ln_statistics(tile, stat_sem, var_sem, n):
                for c in range(TC):
                    nc.vector.bn_stats(stats[:, 6 * c:6 * c + 6], tile[:, c, :]).then_inc(stat_sem, 1)
                dve.wait_ge(stat_sem, (TC + TC) * n + TC)
                dve.sem_inc(passed, 1)
                for c in range(TC):
                    nc.vector.bn_aggr(mv[:, 2 * c:2 * c + 2], stats[:, 6 * c:6 * c + 6]).then_inc(stat_sem, 1)
                dve.wait_ge(stat_sem, (TC + TC) * (n + 1))
                nc.vector.tensor_scalar(var_eps, mv.rearrange("p (c s) -> p c s", s=2)[:, :, 1], EPS, None, ALU.add
                                        ).then_inc(var_sem, 1)

            def normalise(dst, tile, done_sem):
                for c in range(TC):
                    nc.vector.tensor_scalar(dst[:, c, :], tile[:, c, :], mv[:, 2 * c:2 * c + 1], rstd[:, c:c + 1],
                                            ALU.subtract, ALU.mult).then_inc(done_sem, 1)

            def split(dst, src, hi_sem, hi_count, done_sem):
                nc.vector.tensor_copy(dst[:, 0:T], src).then_inc(hi_sem, 1)
                dve.wait_ge(hi_sem, hi_count)
                nc.vector.tensor_tensor(dst[:, T:2 * T], src, dst[:, 0:T], ALU.subtract).then_inc(done_sem, 1)

            def scales(lo, hi):
                r = slice(lo, hi)
                done(nc.vector.tensor_scalar(bound[:, r], bound[:, r], 2.0 ** -100, 2.0 ** 100, ALU.max, ALU.min))
                done(nc.vector.tensor_scalar(pow2[:, r].bitcast(I32), bound[:, r].bitcast(I32), EXPONENT, None,
                                             ALU.bitwise_and))
                done(nc.vector.reciprocal(recip2[:, r], pow2[:, r]))
                done(nc.vector.tensor_scalar(scale[:, r], recip2[:, r], TOP, None, ALU.mult))
                done(nc.vector.tensor_scalar(unscale[:, r], pow2[:, r], 1.0 / TOP, None, ALU.mult))

            def col(tile, i):
                return tile[:, i:i + 1]

            done(nc.vector.memset(zero_col, 0.0))
            done(nc.vector.memset(peaks, 0.0))
            dve.wait_ge(silu_done, 2)
            nc.vector.tensor_tensor(silu_c, silu_c, ct, ALU.mult).then_inc(silu_done, 1)
            dve.wait_ge(silu_done, 3)
            done(nc.vector.tensor_scalar(dec, dec, 1e-7, None, ALU.max))
            for c in range(KC):
                done(nc.vector.memset(decay_pow[:, c, 0:1], 1.0))
                done(nc.vector.tensor_tensor_scan(decay_pow[:, c, 1:T], col(dec, c).to_broadcast([P, T - 1]),
                                                  zero_col.to_broadcast([P, T - 1]), 1.0, ALU.mult, ALU.add))
            for c in range(KC):
                done(nc.vector.tensor_tensor(col(d_tile, c), decay_pow[:, c, T - 1:T], col(dec, c), ALU.mult))
            done(nc.vector.memset(fac[:, 0:KC], 1e10))
            for t in range(1, TPB):
                done(nc.vector.tensor_tensor(fac[:, KC * t:KC * (t + 1)], fac[:, KC * (t - 1):KC * t], d_tile, ALU.mult))
            dve.wait_ge(xa_in, 16)
            ln_statistics(xa, ln_stat, ln_var, 0)
            for i in range(4):
                dve.wait_ge(watt_in[i], 16)
                done(nc.vector.tensor_reduce(col(block_peaks, i), watt_stage[i].rearrange("p a b -> p (a b)"), AX.X,
                                             ALU.max, apply_absolute_value=True))
            done(nc.vector.tensor_reduce(col(peaks, 0), block_peaks[:, 0:4], AX.X, ALU.max))
            for i in (1, 2):
                done(nc.vector.tensor_reduce(col(peaks, 4 + i), cols[:, KC * i:KC * (i + 1)], AX.X, ALU.max,
                                             apply_absolute_value=True))
            dve.wait_ge(ln_rstd, 1)
            normalise(xa, xa, ln_done)
            for i, v in enumerate((SA, CA, SB, CB)):
                dve.wait_ge(modt_ready, i + 1)
                done(nc.vector.tensor_scalar(mod_t[i], ps[4 + i][:, 0:KC * NB], float(v in (CA, CB)), None, ALU.add))
                nc.vector.tensor_reduce(col(peaks, 1 + i), mod_t[i], AX.X, ALU.max, apply_absolute_value=True
                                        ).then_inc(peaks_done, 1)
            dve.wait_ge(peak_all, 1)
            done(nc.vector.tensor_copy(col(bound, S_ATT), col(peak, 0)))
            for s_col, weight, a, b_ in ((S_H1, 23.0, 2, 1), (S_H2, 23.0, 4, 3), (S_N, 1024.0, 5, 6)):
                done(nc.vector.scalar_tensor_tensor(out=col(bound, s_col), in0=col(peak, a), scalar=weight,
                                                    in1=col(peak, b_), op0=ALU.mult, op1=ALU.add))
            scales(0, 4)
            done(nc.vector.tensor_tensor(un_qkv, col(unscale, S_ATT), col(unscale, S_H1), ALU.mult))
            done(nc.vector.tensor_tensor(un_o, col(unscale, S_ATT), col(unscale, S_N), ALU.mult))
            done(nc.vector.tensor_scalar(gn_w_scaled, cols[:, KC:2 * KC], col(scale, S_N), None, ALU.mult))
            done(nc.vector.tensor_scalar(gn_b_scaled, cols[:, 2 * KC:3 * KC], col(scale, S_N), None, ALU.mult))
            for norm in range(2):
                for dst, v in ((ln_b, 2 * norm), (ln_a, 2 * norm + 1)):
                    nc.vector.tensor_scalar(
                        dst[:, norm * NB * KC:(norm + 1) * NB * KC].rearrange("p (b c) -> p b c", b=NB),
                        mod_t[v].rearrange("p (c b) -> p b c", b=NB), col(scale, S_H1 + norm), None, ALU.mult
                        ).then_inc(scales_done, 1)
            for c in range(KC):
                dve.wait_ge(h1_read, c + 1)
                split(h1t[0][:, c, :], h_tmp[:, c % 2, :], h1_hi, c + 1, h1_done)
            dve.wait_ge(mod_copied, 6)
            for i, v in enumerate((GA, GB)):
                waits(dve, gates_done, i)
                g = mod_rows[0:NB, v * D:(v + 1) * D]
                t0, t1 = row_tmp[0:NB, 0, :], row_tmp[0:NB, 1, :]
                done(nc.vector.tensor_scalar(t0, g, -1.0, None, ALU.mult))
                done(nc.vector.tensor_tensor(t0, g, t0, ALU.max))
                done(nc.vector.tensor_scalar(t0, t0, 0.25, None, ALU.max))
                done(nc.vector.tensor_scalar(t1, g, 0.0, 2.0, ALU.is_ge, ALU.mult))
                done(nc.vector.tensor_scalar(t1, t1, -1.0, None, ALU.add))
                nc.vector.tensor_tensor(g, t0, t1, ALU.mult).then_inc(gates_done, 1)
            dve.wait_ge(gates_done, 2)

            def phase1(b, qkv, wo, prep, last=False):
                for t in range(TPB):
                    n = b * TPB + t
                    ln_next = qkv and not (last and t == TPB - 1)
                    if ln_next:
                        dve.wait_ge(xa_in, 16 * (n + 2))
                        ln_statistics(xa, ln_stat, ln_var, n + 1)
                    if wo:
                        dve.wait_ge(wo_ready, TC * n)
                        for c in range(KC):
                            dve.wait_ge(n_read, KC * n + c + 1)
                            split(n_t[:, c, :], n_tmp[:, c % 2, :], n_hi, KC * (n - TPB) + c + 1, n_done)
                    if prep == "none" and t == 2:
                        dve.wait_ge(x1_in[0], 16)
                        ln_statistics(x1[0], ln2_stat, ln2_var, 0)
                        dve.wait_ge(ln2_rstd, 1)
                        dve.wait_ge(prep2_out, 32 * TPB)
                        normalise(xh, x1[0], ln2_done)
                    if prep == "none" and t == 3:
                        for c in range(KC):
                            dve.wait_ge(h2_read, c + 1)
                            split(h2t[0][:, c, :], h2_tmp[:, c % 2, :], h2_hi, c + 1, h2_done)
                    if ln_next:
                        dve.wait_ge(ln_rstd, n + 2)
                        normalise(xa, xa, ln_done)
                    if qkv:
                        for c in range(KC):
                            g = KC * n + c
                            if not (isinstance(g, int) and g < 2):
                                dve.wait_ge(wkv_done, g - 1)
                            nc.vector.tensor_scalar(w_buf[:, c % 2, :], decay_pow[:, c, :], col(fac, KC * t + c), 1.0,
                                                    ALU.mult, ALU.min).then_inc(w_done, 1)
                            dve.wait_ge(k_ready, g + 1)
                            dve.wait_ge(v_read, g + 1)
                            nc.vector.scalar_tensor_tensor(out=kv_buf[:, c % 2, :], in0=ps[bank_rkv(c, 1)][:, :],
                                                           scalar=un_qkv, in1=kv_buf[:, c % 2, :], op0=ALU.mult,
                                                           op1=ALU.mult).then_inc(kv_done, 1)
                            dve.wait_ge(kv_done, g + 1)
                            dve.wait_ge(w_done, g + 1)
                            nc.vector.tensor_tensor(kv_buf[:, c % 2, :], kv_buf[:, c % 2, :], w_buf[:, c % 2, :],
                                                    ALU.mult).then_inc(wkv_done, 1)
                            dve.wait_ge(wkv_done, g + 1)
                            if not (isinstance(g, int) and g < KC):
                                dve.wait_ge(out_done, g - KC + 1)
                                dve.wait_ge(state_done, g - KC + 1)
                            nc.vector.tensor_tensor_scan(state[:, c, :], col(dec, c).to_broadcast([P, T]),
                                                         kv_buf[:, c % 2, :],
                                                         0.0 if t == 0 else state[:, c, T - 1:T], ALU.mult, ALU.add
                                                         ).then_inc(state_done, 1)
                            if c > 0:
                                dve.wait_ge(out_done, g)
                                nc.vector.bn_stats(gn_stats[:, 6 * (KC * t + c - 1):6 * (KC * t + c)],
                                                   slots[:, KC * t + c - 1, :]).then_inc(out_stat, 1)
                            if c == 1 and ln_next:
                                for i in range(KC):
                                    dve.wait_ge(h1_read, KC * (n + 1) + i + 1)
                                    split(h1t[(t + 1) % 2][:, i, :], h_tmp[:, i % 2, :], h1_hi, KC * (n + 1) + i + 1,
                                          h1_done)
                        c = KC - 1
                        dve.wait_ge(out_done, KC * n + KC)
                        nc.vector.bn_stats(gn_stats[:, 6 * (KC * t + c):6 * (KC * t + c + 1)], slots[:, KC * t + c, :]
                                           ).then_inc(out_stat, 1)
                        if t == TPB - 1:
                            dve.wait_ge(out_stat, KC * (n + 1))
                            dve.sem_inc(passed, 1)
                            nc.vector.bn_aggr(gn_mv, gn_stats).then_inc(gn_mv_done, 1)
                    if prep == "max":
                        for i in range(3 * t, 3 * t + 3):
                            dve.wait_ge(max_in[i % 2], 16 * (i // 2 + 1))
                            nc.vector.tensor_reduce(col(block_peaks, i), (stage_a, stage_b)[i % 2], AX.X, ALU.max,
                                                    apply_absolute_value=True).then_inc(block_peak, 1)
                    if wo:
                        for c in range(TC):
                            dve.wait_ge(wo_ready, TC * n + c + 1)
                            dve.wait_ge(x1_done, TC * n + c - 1)
                            dve.wait_ge(gate_a_in, 16)
                            nc.vector.scalar_tensor_tensor(
                                out=o_tmp[:, c % 2, :], in0=ps[c][:, :], scalar=un_o, in1=gate_row(gate_a, b - 1),
                                op0=ALU.mult, op1=ALU.mult).then_inc(wo_read, 1)

            def gate_row(tile, b):
                return tile.rearrange("p b d -> p (b d)")[:, bass.ds(b * D, D)]

            phase1(0, True, False, "max")
            dve.wait_ge(block_peak, 3 * KC)
            nc.vector.tensor_reduce(later_own[:, 0:1], block_peaks[:, 0:2 * KC], AX.X, ALU.max).then_inc(block_peak, 1)
            nc.vector.tensor_reduce(later_own[:, 1:2], block_peaks[:, 2 * KC:3 * KC], AX.X, ALU.max).then_inc(block_peak, 1)
            dve.wait_ge(later_all, 1)
            done(nc.vector.tensor_copy(col(bound, S_FFN), later_peak[:, 0:1]))
            done(nc.vector.tensor_scalar(col(bound, S_W2), later_peak[:, 1:2], 64.0, None, ALU.mult))
            done(nc.vector.tensor_tensor(col(bound_tmp, 0), col(peak, 3), col(peak, 4), ALU.add))
            done(nc.vector.tensor_scalar(col(bound_tmp, 1), col(bound_tmp, 0), later_peak[:, 0:1], 520.0, ALU.mult, ALU.mult))
            done(nc.vector.tensor_scalar(col(bound_tmp, 2), col(bound_tmp, 1), 2.0 ** 50, None, ALU.min))
            done(nc.vector.tensor_tensor(col(bound, S_HID), col(bound_tmp, 2), col(bound_tmp, 2), ALU.mult))
            scales(4, 7)
            done(nc.vector.tensor_tensor(un_gate, col(unscale, S_FFN), col(unscale, S_H2), ALU.mult))
            done(nc.vector.tensor_tensor(un_up, un_gate, col(scale, S_HID), ALU.mult))
            done(nc.vector.tensor_tensor(un_w2, col(unscale, S_HID), col(unscale, S_W2), ALU.mult))
            nc.vector.tensor_scalar(w2_scale, col(scale, S_W2), float(H) ** -0.5, None, ALU.mult).then_inc(later_scales, 1)
            with dve.Fori(1, 3) as b:
                phase1(b, True, True, "w13")
            phase1(3, True, True, "w2", last=True)
            phase1(4, False, True, "none")

            def phase2(s, i, more, b):
                for k in SLOTS:
                    if isinstance(k, str):
                        if more:
                            for c in ((0, 1) if k == "t0" else (2, 3)):
                                dve.wait_ge(h2_read, KC * (s + 1) + c + 1)
                                split(h2t[1 - i][:, c, :], h2_tmp[:, c % 2, :], h2_hi, KC * (s + 1) + c + 1, h2_done)
                        continue
                    g = s * HC + k
                    buf = hid32[:, k % 2, :]
                    dve.wait_ge(sig_done, g + 1)
                    nc.vector.scalar_tensor_tensor(out=buf, in0=ps[bank_ffn(k)][:, :], scalar=un_gate, in1=buf,
                                                   op0=ALU.mult, op1=ALU.mult).then_inc(gated, 1)
                    dve.wait_ge(up_ready, g + 1)
                    dve.wait_ge(gated, g + HC + 1)
                    nc.vector.scalar_tensor_tensor(out=buf, in0=ps[bank_ffn(k) + 1][:, :], scalar=un_up, in1=buf,
                                                   op0=ALU.mult, op1=ALU.mult).then_inc(hid_done, 1)
                    if k == 4 and more:
                        dve.wait_ge(x1_in[1 - i], x1_count(s, i))
                        ln_statistics(x1[1 - i], ln2_stat, ln2_var, s + 1)
                    if k == 6 and more:
                        dve.wait_ge(ln2_rstd, s + 2)
                        normalise(xh, x1[1 - i], ln2_done)
                    dve.wait_ge(hid_hi, g + 1)
                    nc.vector.tensor_tensor(hid16[:, k % 2, T:2 * T], buf, hid16[:, k % 2, 0:T], ALU.subtract
                                            ).then_inc(hid_split, 1)
                for c in range(TC):
                    dve.wait_ge(acc_ready, TC * (s + 1) + c + 1)
                    dve.wait_ge(y_done, TC * (s + 1) + c - 1)
                    dve.wait_ge(gate_b_in, 16)
                    nc.vector.scalar_tensor_tensor(out=f_tmp[:, c % 2, :], in0=ps[c][:, :], scalar=un_w2,
                                                   in1=gate_row(gate_b, b), op0=ALU.mult, op1=ALU.mult).then_inc(acc_read, 1)

            def x1_count(s, i):
                return (s - i) * 8 + (16 if i == 0 else 32)

            with dve.Fori(0, NT // 2 - 1) as pair:
                phase2(pair * 2, 0, True, pair * 2 // TPB)
                phase2(pair * 2 + 1, 1, True, pair * 2 // TPB)
            phase2(NT - 2, 0, True, NB - 1)
            phase2(NT - 1, 1, False, NB - 1)

        @block.tensor
        def _(pe):
            def product(psum, pairs, width):
                for i, (a_hi, a_lo, b_hi, b_lo) in enumerate(pairs):
                    nc.tensor.matmul(psum, a_hi, b_hi, start=(i == 0), stop=False)
                    nc.tensor.matmul(psum, a_hi, b_lo, start=False, stop=False)
                    last = nc.tensor.matmul(psum, a_lo, b_hi, start=False, stop=(i == len(pairs) - 1))
                return last

            def transposes(dst_bank, src, c):
                for i in range(TC):
                    last = nc.tensor.transpose(ps[dst_bank][:, P * i:P * (i + 1)], src[:, i, P * c:P * (c + 1)], ident)
                return last

            pe.wait_ge(silu_done, 3)
            for v in (SA, CA, GA, SB, CB, GB):
                pe.wait_ge(wmod_in[v // 2], 16)
                if v >= 4:
                    pe.wait_ge(mod_copied, v - 3)
                for k in range(KC):
                    at = (v % 4) * D
                    last = nc.tensor.matmul(ps[v % 4][0:NB, :], silu_c[:, NB * k:NB * (k + 1)], wmod_sb[:, k, at:at + D],
                                            start=(k == 0), stop=(k == KC - 1))
                last.then_inc(mod_ready, 1)
            for i, v in enumerate((SA, CA, SB, CB)):
                pe.wait_ge(mod_copied, v + 1)
                for c in range(KC):
                    last = nc.tensor.transpose(ps[4 + i][:, NB * c:NB * (c + 1)],
                                               mod_rows[0:NB, v * D + P * c:v * D + P * (c + 1)], ident[0:NB, 0:NB])
                last.then_inc(modt_ready, 1)
            pe.wait_ge(mod_copied, 6)
            pe.wait_ge(ln_done, TC)
            for c in range(KC):
                transposes(c, xa, c).then_inc(t1_ready, 1)
            pe.wait_ge(peaks_done, 4)
            pe.wait_ge(wsplit, 4)

            def hadamard_slice(t):
                pe.wait_ge(butterfly, 8 * (t + 1))
                for i in range(4):
                    nc.tensor.matmul(ps[i][:, :], had, stage_a[:, T * i:T * (i + 1)], start=True, stop=True
                                     ).then_inc(had_ready, 1)

            def phase1(b, qkv, wo, prep, last=False):
                for t in range(TPB):
                    n = b * TPB + t
                    t1_next = qkv and not (last and t == TPB - 1)
                    if qkv:
                        h = h1t[t % 2]
                        pe.wait_ge(h1_done, KC * (n + 1))
                        for c in range(KC):
                            g = KC * n + c
                            for o, (matrix, ready) in enumerate(((0, v_ready), (1, k_ready), (2, r_ready))):
                                if o == 0 and not (isinstance(g, int) and g < 2):
                                    pe.wait_ge(r_read, g - 1)
                                if o == 1 and not (isinstance(g, int) and g < 1):
                                    pe.wait_ge(v_read, g)
                                if o == 2 and not (isinstance(g, int) and g < 1):
                                    pe.wait_ge(kv_done, g)
                                product(ps[bank_rkv(c, o)][:, :],
                                        [(w_rkv[:, KC * matrix + k, P * c:P * (c + 1)],
                                          w_rkv[:, KC * matrix + k, D + P * c:D + P * (c + 1)],
                                          h[:, k, 0:T], h[:, k, T:2 * T]) for k in range(KC)], T).then_inc(ready, 1)
                            if c == 1 and t1_next:
                                pe.wait_ge(ln_done, TC * (n + 2))
                                if wo:
                                    pe.wait_ge(wo_read, TC * n)
                                for i in range(KC):
                                    transposes(i, xa, i).then_inc(t1_ready, 1)
                            if c == 2 and prep == "w2" and t > 0:
                                if t1_next:
                                    pe.wait_ge(h1_read, KC * (n + 2))
                                else:
                                    pe.wait_ge(wo_read, TC * n)
                                hadamard_slice(t - 1)
                    if prep == "none" and t == 0:
                        pe.wait_ge(wo_read, TC * n)
                        hadamard_slice(TPB - 1)
                    if prep == "none" and t == 3:
                        pe.wait_ge(ln2_done, TC)
                        pe.wait_ge(r_read, KC * NT)
                        for c in range(KC):
                            transposes(4 + c, xh, c).then_inc(t2_ready, 1)
                    if wo:
                        pe.wait_ge(n_done, KC * (n + 1))
                        if t1_next:
                            pe.wait_ge(h1_read, KC * (n + 2))
                        if prep == "w2" and t > 0:
                            pe.wait_ge(had_read, 4 * t)
                        if prep == "none":
                            pe.wait_ge(had_read, 4 * TPB)
                        for c in range(TC):
                            pe.wait_ge(wo_read, TC * (n - 1) + c + 1)
                            product(ps[c][:, :],
                                    [(n_t[:, k, P * c:P * (c + 1)], n_t[:, k, T + P * c:T + P * (c + 1)],
                                      w_o[:, k, 0:D], w_o[:, k, D:2 * D]) for k in range(KC)], D).then_inc(wo_ready, 1)

            phase1(0, True, False, "max")
            with pe.Fori(1, 3) as b:
                phase1(b, True, True, "w13")
            phase1(3, True, True, "w2", last=True)
            phase1(4, False, True, "none")

            pe.wait_ge(w13_in, 16 * 2 * KC)
            pe.wait_ge(h2_done, KC)
            pe.wait_ge(wo_read, TC * (NT + TPB))

            def phase2(s, i, more):
                h = h2t[i]

                def down(k):
                    g = s * HC + k
                    pe.wait_ge(hid_hi, g + 1)
                    pe.wait_ge(hid_split, g + HC + 1)
                    for c in range(TC):
                        if k == 0:
                            pe.wait_ge(acc_read, TC * s + c + 1)
                        hi, lo = hid16[:, k % 2, P * c:P * (c + 1)], hid16[:, k % 2, T + P * c:T + P * (c + 1)]
                        w_hi, w_lo = w2_sb[:, k, 0:D], w2_sb[:, k, D:2 * D]
                        nc.tensor.matmul(ps[c][:, :], hi, w_hi, start=(k == 0), stop=False)
                        nc.tensor.matmul(ps[c][:, :], hi, w_lo, start=False, stop=False)
                        last = nc.tensor.matmul(ps[c][:, :], lo, w_hi, start=False, stop=(k == HC - 1))
                        if k == HC - 1:
                            last.then_inc(acc_ready, 1)
                    if k < HC - 1:
                        last.then_inc(w2_used, 1)

                before = None
                for j, k in enumerate(SLOTS):
                    bank = bank_ffn(k)
                    prior = SLOTS[j - 2]
                    if isinstance(prior, str) and more:
                        pe.wait_ge(h2_read, KC * (s + 1) + (2 if prior == "t0" else 4))
                    elif isinstance(prior, int):
                        pe.wait_ge(hid_done, s * HC + (prior + 1 if j < 2 else HC + prior + 1))
                    else:
                        pe.wait_ge(hid_done, s * HC + HC + SLOTS[j - 4] + 1)
                    if isinstance(k, str):
                        if more:
                            if k == "t0":
                                pe.wait_ge(ln2_done, TC * (s + 2))
                            for x_, c in enumerate((0, 1) if k == "t0" else (2, 3)):
                                transposes(bank + x_, xh, c).then_inc(t2_ready, 1)
                        continue
                    if k == 0:
                        pe.wait_ge(h2_done, KC * (s + 1))
                    for matrix, ready in ((0, gate_ready), (1, up_ready)):
                        product(ps[bank + matrix][:, :],
                                [(w13_sb[:, KC * matrix + c, P * k:P * (k + 1)],
                                  w13_sb[:, KC * matrix + c, H + P * k:H + P * (k + 1)],
                                  h[:, c, 0:T], h[:, c, T:2 * T]) for c in range(KC)], T).then_inc(ready, 1)
                    if before is not None:
                        down(before)
                    before = k
                down(before)

            pe.wait_ge(w2_in, 16)
            with pe.Fori(0, NT // 2 - 1) as pair:
                phase2(pair * 2, 0, True)
                phase2(pair * 2 + 1, 1, True)
            phase2(NT - 2, 0, True)
            phase2(NT - 1, 1, False)


def kernel(L0_attn_x, L0_attn_Wr, L0_attn_Wk, L0_attn_Wv, L0_attn_Wo, L0_attn_decay, L0_attn_gn_weight, L0_attn_gn_bias,
           L0_ffn_W1, L0_ffn_W2, L0_ffn_W3, L0_c, L0_wmod):
    import concourse.bacc as bacc
    from concourse.bass_utils import run_bass_kernel_spmd

    def a(v):
        return np.asarray(v)

    def column(v):
        return a(v).reshape(KC, P).T

    had = np.ones((1, 1), np.float32)
    while had.shape[0] < P:
        had = np.block([[had, had], [had, -had]])
    arrays = {
        "x": a(L0_attn_x).reshape(NB * SEQ, D),
        "w_att": np.stack([a(L0_attn_Wv).T, a(L0_attn_Wk).T, a(L0_attn_Wr).T, a(L0_attn_Wo).T]),
        "w13": np.stack([a(L0_ffn_W1).T, a(L0_ffn_W3).T]),
        "w2t": a(L0_ffn_W2).T,
        "c_t": a(L0_c).T.reshape(KC, P, NB).transpose(1, 0, 2).reshape(P, KC * NB),
        "w_mod": a(L0_wmod),
        "columns": np.concatenate([column(L0_attn_decay), column(L0_attn_gn_weight), column(L0_attn_gn_bias)], axis=1),
        "identity": np.eye(P, dtype=np.float32),
        "hadamard": had,
    }
    arrays = {k: np.ascontiguousarray(v) for k, v in arrays.items()}
    nc = bacc.Bacc("TRN2", target_bir_lowering=False, num_devices=1)
    args = [nc.dram_tensor(k, v.shape, F32, kind="ExternalInput").ap() for k, v in arrays.items()]
    args.append(nc.dram_tensor("out", [NB * SEQ, D], F32, kind="ExternalOutput").ap())
    adaln_block_kernel(nc, *args)
    result = run_bass_kernel_spmd(nc, [arrays], core_ids=[0])
    return result.results[0]["out"].reshape(NB, SEQ, D)
```

```python
from contextlib import ExitStack

import numpy as np

import concourse.bass as bass
from concourse import mybir

ALU = mybir.AluOpType
ACT = mybir.ActivationFunctionType
AX = mybir.AxisListType
F32 = mybir.dt.float32
F16 = mybir.dt.float16
I32 = mybir.dt.int32
RMAX = bass.bass_isa.ReduceOp.max
RADD = bass.bass_isa.ReduceOp.add

P = 128
NB, SEQ, D, H = 4, 2048, 512, 2048
T = 512
TPB = SEQ // T
NT = NB * TPB
KC = D // P
TC = T // P
HC = H // P
EPS = 1e-5
EXPONENT = 0x7F800000
TOP = 2.0 ** 14
SA, CA, GA, SB, CB, GB = range(6)
S_ATT, S_H1, S_N, S_O, S_H2, S_FFN, S_W2, S_HID = range(8)
SLOTS = [*range(10), "t0", 10, 11, "t1", *range(12, HC)]


def waits(eng, sem, count):
    if not isinstance(count, int) or count > 0:
        eng.wait_ge(sem, count)


def adaln_block_kernel(nc, x, w_att, w13, w2t, c_t, w_mod, columns, identity, hadamard, out):
    with ExitStack() as ctx:
        def sem(name):
            return ctx.enter_context(nc.semaphore(name))

        arena = ctx.enter_context(nc.sbuf_tensor("arena", [P, 206 * 256], F32))

        def place(kb, shape, dt=F32):
            n = int(np.prod(shape[1:]))
            words = n if dt == F32 else n // 2
            at = int(kb * 256)
            view = arena[:, at:at + words]
            if dt != F32:
                view = view.bitcast(dt)
            if len(shape) == 3:
                view = view.rearrange("p (a b) -> p a b", a=shape[1])
            if len(shape) == 4:
                view = view.rearrange("p (a b c) -> p a b c", a=shape[1], b=shape[2])
            return view

        w_rkv = place(0, [P, 3 * KC, 2 * D], F16)
        h1t = [place(24 + 8 * i, [P, KC, 2 * T], F16) for i in range(2)]
        xa = place(40, [P, TC, D])
        decay_pow = place(48, [P, KC, T])
        state = place(56, [P, KC, T])
        r_buf = place(64, [P, KC, T])
        kv_buf = place(72, [P, 2, T])
        w_buf = place(76, [P, 2, T])
        h_tmp = place(80, [P, 2, T])
        stage_a = place(86, [P, 2048])
        stage_b = place(94, [P, 2048])
        stage_h = place(102, [P, 2, 2048], F16)
        w_o = place(110, [P, KC, 2 * D], F16)
        slots = place(118, [P, TPB * KC, T])
        n_t = place(150, [P, KC, 2 * T], F16)
        xr = [place(158 + 8 * i, [P, TC, D]) for i in range(2)]
        n_tmp = place(174, [P, 2, T])
        o_tmp = place(178, [P, 2, D])
        gate_a = place(182, [P, NB, D])
        small = place(190, [P, 512])
        w13_sb = place(0, [P, KC, 2 * KC * 2, T], F16)
        w2_sb = place(64, [P, HC, 2 * D], F16)
        xh = place(96, [P, TC, D])
        hid32 = place(104, [P, 2, T])
        h2t = [place(192, [P, KC, 2 * T], F16), place(118, [P, KC, 2 * T], F16)]
        x1 = [place(126, [P, TC, D]), place(134, [P, TC, D])]
        hid16 = place(142, [P, 2, 2 * T], F16)
        h2_tmp = place(146, [P, 2, T])
        f_tmp = place(200, [P, 2, D])
        gate_b = place(182, [P, NB, D])
        wmod_first = place(118, [P, KC, 2 * D])
        wmod_rest = place(134, [P, KC, 4 * D])
        mod_rows = place(192, [P, 6 * D])
        row_tmp = place(174, [P, 4, D])
        watt_stage = [xr[0], xr[1], stage_a.rearrange("p (a b) -> p a b", a=KC),
                      place(126, [P, KC, D])]
        ident = place(204, [P, P])
        had = place(204.5, [P, P])

        used = [0]

        def few(n):
            used[0] += n
            assert used[0] <= 512
            return small[:, used[0] - n:used[0]]

        cols = few(3 * KC)
        ct, silu_c = few(KC * NB), few(KC * NB)
        mod_t = [few(KC * NB) for _ in range(4)]
        ln_a, ln_b = few(2 * NB * KC), few(2 * NB * KC)
        peaks, block_peaks, peaks_o, peak_o = few(8), few(12), few(1), few(1)
        peak, later_peak, later_own = few(8), few(4), few(4)
        bound, pow2, recip2, scale, unscale = few(8), few(8), few(8), few(8), few(8)
        bound_tmp, w2_scale = few(4), few(1)
        un_qkv, un_o, un_gate, un_up, un_w2 = few(1), few(1), few(1), few(1), few(1)
        dec, d_tile = few(KC), few(KC)
        fac = few(TPB * KC)
        zero_col = few(1)
        stats, mv = few(TC * 6), few(TC * 2)
        var_eps, rstd, neg_half = few(TC), few(TC), few(TC)
        gn_stats, gn_mv = few(TPB * KC * 6), few(2)
        gn_all, gn_mean, gn_dev, gn_dev2, gn_sum, gn_sum_all = few(1), few(1), few(1), few(1), few(1), few(1)
        gn_var, gn_rstd = few(1), few(1)
        gn_a, gn_b, gn_mw = few(KC), few(KC), few(KC)
        gn_w_scaled, gn_b_scaled = few(KC), few(KC)

        def coef(tile, norm, b, c):
            return tile[:, bass.ds(norm * NB * KC + b * KC + c, 1)]

        ps = [ctx.enter_context(nc.psum_tensor(f"bank{i}", [P, 512], F32)) for i in range(8)]

        def bank_rkv(c, o):
            return 4 + (3 * c + o) % 4

        def bank_mod(v):
            return 4 + v if v < GA else v - GA

        def bank_mod_t(i):
            return 6 + i if i < 2 else i - 2

        def bank_wo(c, t, qkv):
            return c if qkv or t % 2 == 1 else TC + c

        def w13_chunk(matrix, c, low, k):
            at = P * (k % (HC // KC))
            return w13_sb[:, k // (HC // KC), 2 * (KC * matrix + c) + low, at:at + P]

        def bank_ffn(k):
            return 4 + 2 * (SLOTS.index(k) % 2)

        gates_dram = nc.dram_tensor("gates_scratch", [2, NB * D], F32).ap()
        x1_dram = nc.dram_tensor("x1_scratch", [NT, P, TC * D], F32).ap()
        w13_dram = nc.dram_tensor("w13_scratch", [KC, P, 2 * KC * 2 * T], F16).ap()
        w13_blocks = w13_dram.rearrange("q p (m c l w) -> m c l p q w", m=2, c=KC, l=2)
        w2_dram = nc.dram_tensor("w2_scratch", [P, HC, 2, D], F16).ap()

        x_tiles = x.rearrange("(n c p) d -> n p c d", c=TC, p=P)
        out_tiles = out.rearrange("(n c p) d -> n p c d", c=TC, p=P)
        w_att_v = w_att.rearrange("m (k p) e -> m p k e", p=P)
        w13_v = w13.rearrange("m (k p) h -> m k p h", p=P)
        w2_rows = w2t.rearrange("(g j p) d -> g p j d", j=KC, p=P)
        w2_cols = w2t.rearrange("(j p) (g d) -> g p j d", p=P, d=P)
        w_mod_v = w_mod.rearrange("(k p) n -> p k n", p=P)

        passed = sem("passed")
        cols_in = sem("cols_in")
        ident_in = sem("ident_in")
        had_in = sem("had_in")
        watt_in = [sem(f"watt_in{i}") for i in range(4)]
        wmod_in = [sem(f"wmod_in{i}") for i in range(3)]
        silu_done = sem("silu_done")
        mod_ready = sem("mod_ready")
        mod_copied = sem("mod_copied")
        modt_ready = sem("modt_ready")
        modt_copied = sem("modt_copied")
        gates_done = sem("gates_done")
        gates_out = sem("gates_out")
        gate_a_in = sem("gate_a_in")
        gate_b_in = sem("gate_b_in")
        dve_step = sem("dve_step")
        peaks_done = sem("peaks_done")
        peak_all = sem("peak_all")
        scales_done = sem("scales_done")
        block_peak = sem("block_peak")
        later_all = sem("later_all")
        later_scales = sem("later_scales")
        whi = sem("whi")
        wsplit = sem("wsplit")
        xa_in = sem("xa_in")
        ln_stat = sem("ln_stat")
        ln_var = sem("ln_var")
        ln_rstd = sem("ln_rstd")
        ln_done = sem("ln_done")
        t1_ready = sem("t1_ready")
        h1_read = sem("h1_read")
        h1_hi = sem("h1_hi")
        h1_done = sem("h1_done")
        v_ready = sem("v_ready")
        k_ready = sem("k_ready")
        r_ready = sem("r_ready")
        v_read = sem("v_read")
        r_read = sem("r_read")
        kv_done = sem("kv_done")
        w_done = sem("w_done")
        wkv_done = sem("wkv_done")
        state_done = sem("state_done")
        out_done = sem("out_done")
        out_stat = sem("out_stat")
        gn_mv_done = sem("gn_mv_done")
        gn_step = sem("gn_step")
        gn_done = sem("gn_done")
        n_read = sem("n_read")
        n_hi = sem("n_hi")
        n_done = sem("n_done")
        n_used = sem("n_used")
        wo_ready = sem("wo_ready")
        wo_read = sem("wo_read")
        x1_done = sem("x1_done")
        xr_in = [sem(f"xr_in{i}") for i in range(2)]
        x1_out = [sem(f"x1_out{i}") for i in range(2)]
        max_in = [sem(f"max_in{i}") for i in range(2)]
        prep_in = sem("prep_in")
        prep_scaled = sem("prep_scaled")
        prep_hi = sem("prep_hi")
        prep_lo = sem("prep_lo")
        prep_out = sem("prep_out")
        prep2_in = sem("prep2_in")
        butterfly = sem("butterfly")
        had_ready = sem("had_ready")
        had_read = sem("had_read")
        prep2_hi = sem("prep2_hi")
        prep2_lo = sem("prep2_lo")
        prep2_out = sem("prep2_out")
        w13_in = [sem(f"w13_in{i}") for i in range(4)]
        w2_in = [sem(f"w2_in{i}") for i in range(4)]
        x1_in = [sem(f"x1_in{i}") for i in range(2)]
        ln2_stat = sem("ln2_stat")
        ln2_var = sem("ln2_var")
        ln2_rstd = sem("ln2_rstd")
        ln2_done = sem("ln2_done")
        t2_ready = sem("t2_ready")
        h2_read = sem("h2_read")
        h2_hi = sem("h2_hi")
        h2_done = sem("h2_done")
        gate_ready = sem("gate_ready")
        up_ready = sem("up_ready")
        sig_done = sem("sig_done")
        gated = sem("gated")
        hid_done = sem("hid_done")
        hid_hi = sem("hid_hi")
        hid_split = sem("hid_split")
        w2_used = sem("w2_used")
        acc_ready = sem("acc_ready")
        acc_read = sem("acc_read")
        y_done = sem("y_done")
        y_out = [sem(f"y_out{i}") for i in range(2)]

        HEAD_START = [(n_read, KC * TPB), (n_done, KC * TPB), (n_used, (KC - 1) * TPB), (wo_ready, TC * TPB),
                      (wo_read, TC * TPB), (x1_done, TC * TPB), (prep_lo, TPB), (prep_out, 32 * TPB),
                      (ln2_stat, TC + TC), (ln2_var, 1), (ln2_rstd, 1), (ln2_done, TC),
                      (t2_ready, KC), (h2_read, KC), (h2_hi, KC), (h2_done, KC),
                      (gated, HC), (hid_done, HC), (hid_split, HC), (w2_used, HC - 1),
                      (acc_ready, TC), (acc_read, TC), (y_done, TC)]

        block = ctx.enter_context(nc.Block())

        @block.sync
        def _(sp):
            sp.dma_start(cols, columns).then_inc(cols_in, 16)
            sp.dma_start(ct, c_t).then_inc(cols_in, 16)
            sp.dma_start(xa, x_tiles[0]).then_inc(xa_in, 16)
            sp.dma_start(wmod_first, w_mod_v[:, :, 0:2 * D]).then_inc(wmod_in[0], 16)
            sp.dma_start(ident, identity).then_inc(ident_in, 16)
            for i in range(3):
                sp.dma_start(watt_stage[i], w_att_v[i]).then_inc(watt_in[i], 16)
            sp.wait_ge(t1_ready, KC)
            sp.dma_start(xa, x_tiles[1]).then_inc(xa_in, 16)
            sp.wait_ge(mod_ready, 2)
            sp.dma_start(watt_stage[3], w_att_v[3]).then_inc(watt_in[3], 16)
            sp.dma_start(had, hadamard).then_inc(had_in, 16)
            sp.wait_ge(wsplit, 1)
            for i in range(2):
                sp.dma_start(wmod_rest[:, :, 2 * D * i:2 * D * (i + 1)], w_mod_v[:, :, 2 * D * (i + 1):2 * D * (i + 2)]
                             ).then_inc(wmod_in[i + 1], 16)

            def gates():
                sp.wait_ge(gates_done, 1)
                for i, v in enumerate((GA, GB)):
                    sp.dma_start(gates_dram[i].rearrange("(b d) -> b d", b=NB), mod_rows[0:NB, v * D:(v + 1) * D]
                                 ).then_inc(gates_out, 16)
                sp.wait_ge(gates_out, 32)
                sp.dma_start(gate_a.rearrange("p b d -> p (b d)"), gates_dram[0:1].to_broadcast([P, NB * D])
                             ).then_inc(gate_a_in, 16)

            def load_block(i):
                if i < 2:
                    sp.wait_ge(wsplit, 3)
                else:
                    sp.wait_ge(block_peak, i - 1)
                stage = (stage_a, stage_b)[i % 2]
                if i < 2 * KC:
                    sp.dma_start(stage, w13_v[i // KC, i % KC]).then_inc(max_in[i % 2], 16)
                else:
                    sp.dma_start(stage.rearrange("p (a b) -> p a b", a=KC), w2_rows[i - 2 * KC]
                                 ).then_inc(max_in[i % 2], 16)

            def phase1(b, wo, prep, last=False):
                for t in range(TPB):
                    n = b * TPB + t
                    if prep == "max" and t < TPB - 1:
                        load_block(KC * t)
                        load_block(KC * t + 1)
                    if prep == "w13":
                        sp.wait_ge(block_peak, 3 * KC)
                        sp.wait_ge(prep_lo, n)
                        sp.dma_start(stage_a, w13_v[b - 1, t]).then_inc(prep_in, 16)
                    if prep == "w2":
                        sp.wait_ge(prep_lo, 3 * TPB)
                        waits(sp, had_ready, 4 * t)
                        sp.dma_start(stage_a.rearrange("p (a b) -> p a b", a=HC), w2_cols[t]).then_inc(prep2_in, 16)
                    if prep != "none" and not (last and t == TPB - 1):
                        sp.wait_ge(t1_ready, KC * (n + 2))
                        if last and t == TPB - 2:
                            sp.dma_start(xa.rearrange("p a b -> p (a b)"), x1_dram[0]).then_inc(xa_in, 16)
                        else:
                            sp.dma_start(xa, x_tiles[n + 2]).then_inc(xa_in, 16)
                    if prep == "max":
                        if t < TPB - 1:
                            load_block(KC * t + 2)
                            load_block(KC * t + 3)
                        if t == 2:
                            gates()
                        if t >= 2:
                            sp.wait_ge(mod_ready, 6)
                            sp.dma_start(xr[t - 2], x_tiles[t - 2]).then_inc(xr_in[t - 2], 16)
                    if prep == "w2" and t > 0:
                        store_w2(t - 1)
                    if last and t == TPB - 1:
                        sp.wait_ge(r_ready, KC * NT)
                        sp.wait_ge(prep_out, 32 * 3 * TPB)
                        for q in range(KC):
                            if q == KC - 1:
                                sp.wait_ge(out_done, KC * NT)
                            sp.dma_start(w13_sb[:, q].rearrange("p i w -> p (i w)"), w13_dram[q]
                                         ).then_inc(w13_in[q], 16)
                    if wo:
                        sp.wait_ge(x1_done, TC * (n + 1))
                        sp.dma_start(x1_dram[n - TPB], xr[t % 2].rearrange("p a b -> p (a b)")
                                     ).then_inc(x1_out[t % 2], 16)
                        sp.wait_ge(x1_out[t % 2], 32 * (b - 1) + 16 * (t // 2 + 1))
                        if prep != "none" or t < 2:
                            sp.dma_start(xr[t % 2], x_tiles[n - 2]).then_inc(xr_in[t % 2], 16)
                    if prep == "w13":
                        sp.wait_ge(prep_lo, n + 1)
                        for i in range(2):
                            sp.dma_start(w13_blocks[b - 1, t, i], stage_h[:, i, :].rearrange("p (q w) -> p q w", q=KC)
                                         ).then_inc(prep_out, 16)
                    if prep == "none" and t == 0:
                        store_w2(TPB - 1)
                        sp.wait_ge(out_stat, KC * NT)
                        sp.wait_ge(h1_done, KC * (NT + 1))
                        sp.wait_ge(prep2_out, 32 * TPB)
                        load_w2(0)
                    if prep == "none" and t == 1:
                        for q in range(1, KC):
                            load_w2(q)
                        for i in (1, 0):
                            sp.wait_ge(n_read, KC * (n + 1 + i))
                            sp.dma_start(x1[i].rearrange("p a b -> p (a b)"), x1_dram[i]).then_inc(x1_in[i], 16)

            def load_w2(q):
                part = slice(q * (HC // KC), (q + 1) * (HC // KC))
                sp.dma_start(w2_sb[:, part].rearrange("p a b -> p (a b)"),
                             w2_dram[:, part].rearrange("p a b c -> p (a b c)")).then_inc(w2_in[q], 16)

            def store_w2(t):
                sp.wait_ge(prep2_lo, t + 1)
                for i in range(2):
                    sp.dma_start(w2_dram[:, :, i, P * t:P * (t + 1)],
                                 stage_h[:, i, :].rearrange("p (a b) -> p a b", a=HC)).then_inc(prep2_out, 16)

            phase1(0, False, "max")
            with sp.Fori(1, 3) as b:
                phase1(b, True, "w13")
            phase1(3, True, "w2", last=True)
            phase1(4, True, "none")

            sp.dma_start(gate_b.rearrange("p b d -> p (b d)"), gates_dram[1:2].to_broadcast([P, NB * D])
                         ).then_inc(gate_b_in, 16)

            def phase2(s, i, more):
                sp.wait_ge(y_done, TC * (s + 2))
                sp.dma_start(out_tiles[s], x1[i]).then_inc(y_out[i], 16)
                if more:
                    sp.wait_ge(y_out[i], (s - i) * 8 + 16)
                    sp.dma_start(x1[i].rearrange("p a b -> p (a b)"), x1_dram[s + 2]).then_inc(x1_in[i], 16)

            with sp.Fori(0, NT // 2 - 1) as pair:
                phase2(pair * 2, 0, True)
                phase2(pair * 2 + 1, 1, True)
            phase2(NT - 2, 0, False)
            for c in range(TC):
                sp.wait_ge(y_done, TC * NT + c + 1)
                sp.dma_start(out_tiles[NT - 1][:, c], x1[1][:, c]).then_inc(y_out[1], 16)
            sp.wait_ge(y_out[0], 16 * NT // 2)
            sp.wait_ge(y_out[1], 16 * (NT // 2 - 1) + 16 * TC)

        @block.gpsimd
        def _(pool):
            for s, count in HEAD_START:
                nc.gpsimd.sem_inc(s, count)
            nc.gpsimd.memset(neg_half, -0.5).then_inc(gn_step, 1)
            pool.wait_ge(gn_step, 1)
            pool.wait_ge(ln_var, 1)
            nc.gpsimd.tensor_tensor(rstd, var_eps, neg_half, ALU.pow).then_inc(ln_rstd, 1)
            pool.wait_ge(peaks_done, 1)
            nc.gpsimd.partition_all_reduce(peak, peaks, P, RMAX).then_inc(peak_all, 1)

            def batch_norm(b):
                def after(i):
                    pool.wait_ge(gn_step, 10 * b + 1 + i)
                    pool.sem_inc(passed, 1)

                pool.wait_ge(gn_mv_done, b + 1)
                pool.sem_inc(passed, 1)
                nc.gpsimd.partition_all_reduce(gn_all, gn_mv[:, 0:1], P, RADD).then_inc(gn_step, 1)
                after(1)
                nc.gpsimd.tensor_scalar(gn_mean, gn_all, 1.0 / P, None, ALU.mult).then_inc(gn_step, 1)
                after(2)
                nc.gpsimd.tensor_tensor(gn_dev, gn_mv[:, 0:1], gn_mean, ALU.subtract).then_inc(gn_step, 1)
                after(3)
                nc.gpsimd.tensor_tensor(gn_dev2, gn_dev, gn_dev, ALU.mult).then_inc(gn_step, 1)
                after(4)
                nc.gpsimd.tensor_tensor(gn_sum, gn_dev2, gn_mv[:, 1:2], ALU.add).then_inc(gn_step, 1)
                after(5)
                nc.gpsimd.partition_all_reduce(gn_sum_all, gn_sum, P, RADD).then_inc(gn_step, 1)
                after(6)
                nc.gpsimd.tensor_scalar(gn_var, gn_sum_all, 1.0 / P, EPS, ALU.mult, ALU.add).then_inc(gn_step, 1)
                after(7)
                nc.gpsimd.tensor_tensor(gn_rstd, gn_var, neg_half[:, 0:1], ALU.pow).then_inc(gn_step, 1)
                after(8)
                pool.wait_ge(n_read, KC * TPB * (b + 1))
                pool.sem_inc(passed, 1)
                nc.gpsimd.tensor_scalar(gn_a, gn_w_scaled, gn_rstd, None, ALU.mult).then_inc(gn_step, 1)
                after(9)
                nc.gpsimd.tensor_scalar(gn_mw, gn_a, gn_mean, None, ALU.mult).then_inc(gn_step, 1)
                after(10)
                nc.gpsimd.tensor_tensor(gn_b, gn_b_scaled, gn_mw, ALU.subtract).then_inc(gn_done, 1)

            def low_w2(t):
                pool.wait_ge(prep2_hi, t + 1)
                if t == 0:
                    pool.wait_ge(prep_out, 32 * 3 * TPB)
                else:
                    pool.wait_ge(prep2_out, 32 * t)
                nc.gpsimd.tensor_tensor(stage_h[:, 1, :], stage_b, stage_h[:, 0, :], ALU.subtract).then_inc(prep2_lo, 1)

            def butterflies(t, i):
                if i > 0:
                    pool.wait_ge(butterfly, 8 * t + 2 * i)
                else:
                    pool.wait_ge(prep2_in, 16 * (t + 1))
                    waits(pool, prep2_lo, t)
                src, dst = (stage_a, stage_b) if i % 2 == 0 else (stage_b, stage_a)
                src = src.rearrange("p (a two h) -> p a two h", two=2, h=P << i)
                dst = dst.rearrange("p (a two h) -> p a two h", two=2, h=P << i)
                nc.gpsimd.tensor_tensor(dst[:, :, 0, :], src[:, :, 0, :], src[:, :, 1, :], ALU.add
                                        ).then_inc(butterfly, 1)
                nc.gpsimd.tensor_tensor(dst[:, :, 1, :], src[:, :, 0, :], src[:, :, 1, :], ALU.subtract
                                        ).then_inc(butterfly, 1)

            def phase1(b, qkv, wo, prep, last=False):
                for t in range(TPB):
                    n = b * TPB + t
                    if qkv:
                        pool.wait_ge(ln_var, n + 2)
                        nc.gpsimd.tensor_tensor(rstd, var_eps, neg_half, ALU.pow).then_inc(ln_rstd, 1)
                        if prep == "max" and t == TPB - 1:
                            pool.wait_ge(block_peak, 3 * KC + 2)
                            nc.gpsimd.partition_all_reduce(later_peak, later_own, P, RMAX).then_inc(later_all, 1)
                        for c in range(KC):
                            if prep == "w2" and c == 1 and t > 0:
                                low_w2(t - 1)
                            pool.wait_ge(r_read, KC * n + c + 1)
                            pool.wait_ge(state_done, KC * n + c + 1)
                            pool.wait_ge(n_read, KC * n + c + 1)
                            if wo:
                                pool.wait_ge(out_stat, KC * (n - TPB) + c + 1)
                            nc.gpsimd.tensor_tensor(slots[:, KC * t + c, :], state[:, c, :], r_buf[:, c, :], ALU.mult
                                                    ).then_inc(out_done, 1)
                            if prep == "max" and t == 0 and c == 1:
                                pool.wait_ge(peaks_done, 2)
                                nc.gpsimd.partition_all_reduce(peak_o, peaks_o, P, RMAX).then_inc(peak_all, 1)
                            if prep == "w2" and c > 0 and not (c == KC - 1 and t == TPB - 1):
                                butterflies(t, c - 1)
                        if t == TPB - 1:
                            batch_norm(b)
                            if prep == "w2":
                                butterflies(t, 2)
                    if last and t == TPB - 1:
                        butterflies(t, 3)
                    if wo:
                        for c in range(TC):
                            pool.wait_ge(wo_read, TC * n + c + 1)
                            pool.wait_ge(xr_in[t % 2], 32 * (b - 1) + 16 * (t // 2 + 1))
                            nc.gpsimd.tensor_tensor(xr[t % 2][:, c, :], xr[t % 2][:, c, :], o_tmp[:, c % 2, :], ALU.add
                                                    ).then_inc(x1_done, 1)
                    if prep == "w13":
                        pool.wait_ge(prep_hi, n - TPB + 1)
                        pool.wait_ge(prep_out, 32 * n)
                        nc.gpsimd.tensor_tensor(stage_h[:, 1, :], stage_a, stage_h[:, 0, :], ALU.subtract
                                                ).then_inc(prep_lo, 1)
                    if prep == "w2" and t < TPB - 1:
                        butterflies(t, 3)
                    if prep == "none" and t == 0:
                        low_w2(TPB - 1)

            phase1(0, True, False, "max")
            with pool.Fori(1, 3) as b:
                phase1(b, True, True, "w13")
            phase1(3, True, True, "w2", last=True)
            phase1(4, False, True, "none")

            def phase2(s, i, more):
                if more:
                    pool.wait_ge(ln2_var, s + 2)
                    nc.gpsimd.tensor_tensor(rstd, var_eps, neg_half, ALU.pow).then_inc(ln2_rstd, 1)
                for c in range(TC):
                    pool.wait_ge(acc_read, TC * (s + 1) + c + 1)
                    nc.gpsimd.tensor_tensor(x1[i][:, c, :], x1[i][:, c, :], f_tmp[:, c % 2, :], ALU.add
                                            ).then_inc(y_done, 1)

            with pool.Fori(0, NT // 2 - 1) as pair:
                phase2(pair * 2, 0, True)
                phase2(pair * 2 + 1, 1, True)
            phase2(NT - 2, 0, True)
            phase2(NT - 1, 1, False)

        @block.scalar
        def _(act):
            def copy(dst, src, scale=1.0):
                return nc.scalar.activation(dst, src, ACT.Copy, scale=scale)

            def modulate1(n, norm, b, chunks=range(KC)):
                for c in chunks:
                    act.wait_ge(t1_ready, KC * n + c + 1)
                    if not (isinstance(n, int) and KC * n + c < 2):
                        act.wait_ge(h1_done, KC * n + c - 1)
                    act.sem_inc(passed, 1)
                    nc.scalar.activation(h_tmp[:, c % 2, :], ps[c][:, :], ACT.Identity, scale=coef(ln_a, norm, b, c),
                                         bias=coef(ln_b, norm, b, c)).then_inc(h1_read, 1)

            def modulate2(b, s, chunks, banks):
                for c, bank in zip(chunks, banks):
                    act.wait_ge(t2_ready, KC * s + c + 1)
                    act.wait_ge(h2_done, KC * s + c - 1)
                    act.sem_inc(passed, 1)
                    nc.scalar.activation(h2_tmp[:, c % 2, :], ps[bank][:, :], ACT.Identity, scale=coef(ln_a, 1, b, c),
                                         bias=coef(ln_b, 1, b, c)).then_inc(h2_read, 1)

            act.wait_ge(cols_in, 32)
            nc.scalar.activation(silu_c, ct, ACT.Sigmoid).then_inc(silu_done, 1)
            nc.scalar.activation(dec, cols[:, 0:KC], ACT.Sigmoid).then_inc(silu_done, 1)

            def copy_mod_rows(vectors):
                for v in vectors:
                    act.wait_ge(mod_ready, v + 1)
                    copy(mod_rows[0:NB, v * D:(v + 1) * D], ps[bank_mod(v)][0:NB, :]).then_inc(mod_copied, 1)

            copy_mod_rows((SA, CA))
            def weight_high(i):
                w = w_rkv[:, KC * i:KC * (i + 1), :] if i < 3 else w_o
                act.wait_ge(scales_done, 1 if i < 3 else 4)
                act.wait_ge(watt_in[i], 16)
                column = S_ATT if i < 3 else S_O
                copy(w[:, :, 0:D], watt_stage[i], scale[:, column:column + 1]).then_inc(whi, 1)

            act.wait_ge(scales_done, 3)
            modulate1(0, 0, 0, (0, 1))
            weight_high(0)
            modulate1(0, 0, 0, (2, 3))
            weight_high(1)
            weight_high(2)

            def split_w2(t):
                for i in range(4):
                    act.wait_ge(had_ready, 4 * t + i + 1)
                    copy(stage_b[:, T * i:T * (i + 1)], ps[i][:, :], w2_scale).then_inc(had_read, 1)
                act.wait_ge(had_read, 4 * t + 4)
                if t == 0:
                    act.wait_ge(prep_out, 32 * 3 * TPB)
                else:
                    act.wait_ge(prep2_out, 32 * t)
                copy(stage_h[:, 0, :], stage_b).then_inc(prep2_hi, 1)

            def normalise_batch(b, t, n):
                for c in range(KC):
                    act.wait_ge(gn_done, b)
                    act.wait_ge(n_done, KC * n + c - 1)
                    nc.scalar.activation(n_tmp[:, c % 2, :], slots[:, KC * t + c, :], ACT.Identity,
                                         scale=gn_a[:, c:c + 1], bias=gn_b[:, c:c + 1]).then_inc(n_read, 1)

            def phase1(b, qkv, wo, prep, last=False):
                for t in range(TPB):
                    n = b * TPB + t
                    if not qkv:
                        normalise_batch(b, t, n)
                        if t == 1:
                            split_w2(TPB - 1)
                        continue
                    if wo and t > 0:
                        normalise_batch(b, t, n)
                    for c in range(KC):
                        g = KC * n + c
                        act.wait_ge(v_ready, g + 1)
                        if not (isinstance(g, int) and g < 2):
                            act.wait_ge(state_done, g - 1)
                        copy(kv_buf[:, c % 2, :], ps[bank_rkv(c, 0)][:, :], un_qkv).then_inc(v_read, 1)
                        act.wait_ge(r_ready, g + 1)
                        if not (isinstance(g, int) and g < 4):
                            act.wait_ge(out_done, g - 3)
                        nc.scalar.activation(r_buf[:, c, :], ps[bank_rkv(c, 2)][:, :], ACT.Sigmoid, scale=un_qkv
                                             ).then_inc(r_read, 1)
                        if c == 0 and prep == "w2" and t > 0:
                            split_w2(t - 1)
                        if c == 1:
                            if last and t == TPB - 1:
                                modulate1(n + 1, 1, 0)
                            else:
                                modulate1(n + 1, 0, b + (t + 1) // TPB)
                        if c == 1 and prep == "max" and t == 0:
                            weight_high(3)
                        if c == 1 and wo and t == 0:
                            normalise_batch(b, t, n)
                    if prep == "max" and t == 0:
                        copy_mod_rows((GA, SB, CB, GB))
                    if prep == "w13":
                        act.wait_ge(later_scales, 1)
                        act.wait_ge(prep_in, 16 * (n - TPB + 1))
                        copy(stage_a, stage_a, scale[:, S_FFN:S_FFN + 1]).then_inc(prep_scaled, 1)
                        act.wait_ge(prep_scaled, n - TPB + 1)
                        act.wait_ge(prep_out, 32 * n)
                        copy(stage_h[:, 0, :], stage_a).then_inc(prep_hi, 1)

            phase1(0, True, False, "max")
            with act.Fori(1, 3) as b:
                phase1(b, True, True, "w13")
            phase1(3, True, True, "w2", last=True)
            phase1(4, False, True, "none")

            act.wait_ge(prep2_out, 32 * TPB)
            act.wait_ge(n_read, KC * (NT + TPB))

            def phase2(s, i, more, b_next):
                for k in SLOTS:
                    if k == "t0" and more:
                        modulate2(b_next, s + 1, (0, 1), (bank_ffn(k), bank_ffn(k) + 1))
                    if k == "t1" and more:
                        modulate2(b_next, s + 1, (2, 3), (bank_ffn(k), bank_ffn(k) + 1))
                    if isinstance(k, str):
                        continue
                    g = s * HC + k
                    act.wait_ge(gate_ready, g + 1)
                    act.wait_ge(hid_split, g + HC - 1)
                    nc.scalar.activation(hid32[:, k % 2, :], ps[bank_ffn(k)][:, :], ACT.Sigmoid, scale=un_gate
                                         ).then_inc(sig_done, 1)
                    act.wait_ge(hid_done, g + HC + 1)
                    if k == 1:
                        act.wait_ge(acc_ready, TC * (s + 1))
                    else:
                        act.wait_ge(w2_used, (s + 1) * (HC - 1) + max(k - 1, 0))
                    copy(hid16[:, k % 2, 0:T], hid32[:, k % 2, :]).then_inc(hid_hi, 1)

            with act.Fori(0, NT // 2 - 1) as pair:
                phase2(pair * 2, 0, True, pair * 2 // TPB)
                phase2(pair * 2 + 1, 1, True, (pair * 2 + 2) // TPB)
            phase2(NT - 2, 0, True, NB - 1)
            phase2(NT - 1, 1, False, None)

        @block.vector
        def _(dve):
            steps = [0]

            def done(instruction):
                steps[0] += 1
                instruction.then_inc(dve_step, 1)
                dve.wait_ge(dve_step, steps[0])

            def ln_statistics(tile, stat_sem, var_sem, n):
                for c in range(TC):
                    nc.vector.bn_stats(stats[:, 6 * c:6 * c + 6], tile[:, c, :]).then_inc(stat_sem, 1)
                dve.wait_ge(stat_sem, (TC + TC) * n + TC)
                dve.sem_inc(passed, 1)
                for c in range(TC):
                    nc.vector.bn_aggr(mv[:, 2 * c:2 * c + 2], stats[:, 6 * c:6 * c + 6]).then_inc(stat_sem, 1)
                dve.wait_ge(stat_sem, (TC + TC) * (n + 1))
                nc.vector.tensor_scalar(var_eps, mv.rearrange("p (c s) -> p c s", s=2)[:, :, 1], EPS, None, ALU.add
                                        ).then_inc(var_sem, 1)

            def normalise(dst, tile, done_sem):
                for c in range(TC):
                    nc.vector.tensor_scalar(dst[:, c, :], tile[:, c, :], mv[:, 2 * c:2 * c + 1], rstd[:, c:c + 1],
                                            ALU.subtract, ALU.mult).then_inc(done_sem, 1)

            def split(dst, src, hi_sem, hi_count, done_sem):
                nc.vector.tensor_copy(dst[:, 0:T], src).then_inc(hi_sem, 1)
                dve.wait_ge(hi_sem, hi_count)
                nc.vector.tensor_tensor(dst[:, T:2 * T], src, dst[:, 0:T], ALU.subtract).then_inc(done_sem, 1)

            def scales(lo, hi):
                r = slice(lo, hi)
                done(nc.vector.tensor_scalar(bound[:, r], bound[:, r], 2.0 ** -100, 2.0 ** 100, ALU.max, ALU.min))
                done(nc.vector.tensor_scalar(pow2[:, r].bitcast(I32), bound[:, r].bitcast(I32), EXPONENT, None,
                                             ALU.bitwise_and))
                done(nc.vector.reciprocal(recip2[:, r], pow2[:, r]))
                done(nc.vector.tensor_scalar(scale[:, r], recip2[:, r], TOP, None, ALU.mult))
                done(nc.vector.tensor_scalar(unscale[:, r], pow2[:, r], 1.0 / TOP, None, ALU.mult))

            def col(tile, i):
                return tile[:, i:i + 1]

            done(nc.vector.memset(zero_col, 0.0))
            done(nc.vector.memset(peaks, 0.0))
            dve.wait_ge(silu_done, 2)
            nc.vector.tensor_tensor(silu_c, silu_c, ct, ALU.mult).then_inc(silu_done, 1)
            done(nc.vector.tensor_scalar(dec, dec, 1e-7, None, ALU.max))
            for c in range(KC):
                done(nc.vector.memset(decay_pow[:, c, 0:1], 1.0))
                done(nc.vector.tensor_tensor_scan(decay_pow[:, c, 1:T], col(dec, c).to_broadcast([P, T - 1]),
                                                  zero_col.to_broadcast([P, T - 1]), 1.0, ALU.mult, ALU.add))
            for c in range(KC):
                done(nc.vector.tensor_tensor(col(d_tile, c), decay_pow[:, c, T - 1:T], col(dec, c), ALU.mult))
            done(nc.vector.memset(fac[:, 0:KC], 1e10))
            for t in range(1, TPB):
                done(nc.vector.tensor_tensor(fac[:, KC * t:KC * (t + 1)], fac[:, KC * (t - 1):KC * t], d_tile,
                                             ALU.mult))

            def weight_peak(dst, i):
                dve.wait_ge(watt_in[i], 16)
                done(nc.vector.tensor_reduce(dst, watt_stage[i].rearrange("p a b -> p (a b)"), AX.X,
                                             ALU.max, apply_absolute_value=True))

            def mod_peak(dst, i):
                dve.wait_ge(modt_ready, i + 1)
                nc.vector.tensor_scalar(mod_t[i], ps[bank_mod_t(i)][:, 0:KC * NB], float(i % 2), None, ALU.add
                                        ).then_inc(modt_copied, 1)
                dve.wait_ge(modt_copied, i + 1)
                done(nc.vector.tensor_reduce(dst, mod_t[i], AX.X, ALU.max, apply_absolute_value=True))

            def coefficients(norm):
                for dst, v in ((ln_b, 2 * norm), (ln_a, 2 * norm + 1)):
                    nc.vector.tensor_scalar(
                        dst[:, norm * NB * KC:(norm + 1) * NB * KC].rearrange("p (b c) -> p b c", b=NB),
                        mod_t[v].rearrange("p (c b) -> p b c", b=NB), col(scale, (S_H1, S_H2)[norm]), None, ALU.mult
                        ).then_inc(scales_done, 1)

            def weight_low(i):
                w = w_rkv[:, KC * i:KC * (i + 1), :] if i < 3 else w_o
                dve.wait_ge(whi, i + 1)
                nc.vector.scalar_tensor_tensor(out=w[:, :, D:], in0=watt_stage[i],
                                               scalar=col(scale, S_ATT if i < 3 else S_O), in1=w[:, :, 0:D],
                                               op0=ALU.mult, op1=ALU.subtract).then_inc(wsplit, 1)

            for i in (1, 2):
                done(nc.vector.tensor_reduce(col(peaks, 2 + i), cols[:, KC * i:KC * (i + 1)], AX.X, ALU.max,
                                             apply_absolute_value=True))
            dve.wait_ge(xa_in, 16)
            ln_statistics(xa, ln_stat, ln_var, 0)
            dve.wait_ge(ln_rstd, 1)
            normalise(xa, xa, ln_done)
            for i in range(3):
                weight_peak(col(block_peaks, i), i)
            for i in range(2):
                mod_peak(col(peaks, 1 + i), i)
            nc.vector.tensor_reduce(col(peaks, 0), block_peaks[:, 0:3], AX.X, ALU.max).then_inc(peaks_done, 1)
            dve.wait_ge(peak_all, 1)
            done(nc.vector.tensor_copy(col(bound, S_ATT), col(peak, 0)))
            for s_col, weight, a, b_ in ((S_H1, 23.0, 2, 1), (S_N, 1024.0, 3, 4)):
                done(nc.vector.scalar_tensor_tensor(out=col(bound, s_col), in0=col(peak, a), scalar=weight,
                                                    in1=col(peak, b_), op0=ALU.mult, op1=ALU.add))
            scales(0, 3)
            nc.vector.tensor_tensor(un_qkv, col(unscale, S_ATT), col(unscale, S_H1), ALU.mult).then_inc(scales_done, 1)
            coefficients(0)
            for c in range(KC):
                if c == 2:
                    weight_low(0)
                dve.wait_ge(h1_read, c + 1)
                split(h1t[0][:, c, :], h_tmp[:, c % 2, :], h1_hi, c + 1, h1_done)
            weight_low(1)
            weight_low(2)
            def output_scale():
                weight_peak(col(block_peaks, 3), 3)
                nc.vector.tensor_copy(peaks_o, col(block_peaks, 3)).then_inc(peaks_done, 1)
                dve.wait_ge(peak_all, 2)
                done(nc.vector.tensor_copy(col(bound, S_O), peak_o))
                scales(3, 4)
                nc.vector.tensor_tensor(un_o, col(unscale, S_O), col(unscale, S_N), ALU.mult).then_inc(scales_done, 1)
                done(nc.vector.tensor_scalar(gn_w_scaled, cols[:, KC:2 * KC], col(scale, S_N), None, ALU.mult))
                done(nc.vector.tensor_scalar(gn_b_scaled, cols[:, 2 * KC:3 * KC], col(scale, S_N), None, ALU.mult))

            def block_maxima():
                dve.wait_ge(block_peak, 3 * KC)
                nc.vector.tensor_reduce(later_own[:, 0:1], block_peaks[:, 0:2 * KC], AX.X, ALU.max
                                        ).then_inc(block_peak, 1)
                nc.vector.tensor_reduce(later_own[:, 1:2], block_peaks[:, 2 * KC:3 * KC], AX.X, ALU.max
                                        ).then_inc(block_peak, 1)

            def ffn_scales():
                dve.wait_ge(later_all, 1)
                done(nc.vector.tensor_copy(col(bound, S_FFN), later_peak[:, 0:1]))
                done(nc.vector.tensor_scalar(col(bound, S_W2), later_peak[:, 1:2], 64.0, None, ALU.mult))
                done(nc.vector.tensor_tensor(col(bound_tmp, 0), later_peak[:, 2:3], later_peak[:, 3:4], ALU.add))
                done(nc.vector.scalar_tensor_tensor(out=col(bound, S_H2), in0=later_peak[:, 3:4], scalar=23.0,
                                                    in1=later_peak[:, 2:3], op0=ALU.mult, op1=ALU.add))
                done(nc.vector.tensor_scalar(col(bound_tmp, 1), col(bound_tmp, 0), later_peak[:, 0:1], 520.0,
                                             ALU.mult, ALU.mult))
                done(nc.vector.tensor_scalar(col(bound_tmp, 2), col(bound_tmp, 1), 2.0 ** 50, None, ALU.min))
                done(nc.vector.tensor_tensor(col(bound, S_HID), col(bound_tmp, 2), col(bound_tmp, 2), ALU.mult))
                scales(4, 8)
                coefficients(1)
                done(nc.vector.tensor_tensor(un_gate, col(unscale, S_FFN), col(unscale, S_H2), ALU.mult))
                done(nc.vector.tensor_tensor(un_up, un_gate, col(scale, S_HID), ALU.mult))
                done(nc.vector.tensor_tensor(un_w2, col(unscale, S_HID), col(unscale, S_W2), ALU.mult))
                nc.vector.tensor_scalar(w2_scale, col(scale, S_W2), float(H) ** -0.5, None, ALU.mult
                                        ).then_inc(later_scales, 1)

            def gates():
                dve.wait_ge(mod_copied, 6)
                g = mod_rows.rearrange("p (three v d) -> p three v d", three=2, v=3)[0:NB, :, GA, :]
                size, sign = row_tmp[0:NB, 0:2, :], row_tmp[0:NB, 2:4, :]
                done(nc.vector.scalar_tensor_tensor(out=size, in0=g, scalar=-1.0, in1=g, op0=ALU.mult, op1=ALU.max))
                done(nc.vector.tensor_scalar(size, size, 0.25, None, ALU.max))
                done(nc.vector.tensor_scalar(sign, g, 0.0, 2.0, ALU.is_ge, ALU.mult))
                nc.vector.scalar_tensor_tensor(out=g, in0=sign, scalar=-1.0, in1=size, op0=ALU.add, op1=ALU.mult
                                               ).then_inc(gates_done, 1)

            def chunk_statistics(n, t, c):
                dve.wait_ge(out_done, KC * n + c + 1)
                nc.vector.bn_stats(gn_stats[:, 6 * (KC * t + c):6 * (KC * t + c + 1)], slots[:, KC * t + c, :]
                                   ).then_inc(out_stat, 1)

            def split_n(n):
                for c in range(KC):
                    if c < KC - 1:
                        dve.wait_ge(n_used, (KC - 1) * (n - 1) + c + 1)
                    else:
                        dve.wait_ge(wo_ready, TC * n)
                    dve.wait_ge(n_read, KC * n + c + 1)
                    split(n_t[:, c, :], n_tmp[:, c % 2, :], n_hi, KC * (n - TPB) + c + 1, n_done)

            def phase1(b, qkv, wo, prep, last=False):
                for t in range(TPB):
                    n = b * TPB + t
                    if prep == "max" and t == TPB - 1:
                        block_maxima()
                    if qkv:
                        dve.wait_ge(xa_in, 16 * (n + 2))
                        ln_statistics(xa, ln_stat, ln_var, n + 1)
                    if prep == "none" and t < TPB - 1:
                        split_n(n + 1)
                    if qkv and wo and t > 0:
                        split_n(n)
                    if qkv:
                        dve.wait_ge(ln_rstd, n + 2)
                        normalise(xa, xa, ln_done)
                    if qkv:
                        for c in range(KC):
                            g = KC * n + c
                            if not (isinstance(g, int) and g < 2):
                                dve.wait_ge(wkv_done, g - 1)
                            nc.vector.tensor_scalar(w_buf[:, c % 2, :], decay_pow[:, c, :], col(fac, KC * t + c), 1.0,
                                                    ALU.mult, ALU.min).then_inc(w_done, 1)
                            dve.wait_ge(k_ready, g + 1)
                            dve.wait_ge(v_read, g + 1)
                            nc.vector.scalar_tensor_tensor(out=kv_buf[:, c % 2, :], in0=ps[bank_rkv(c, 1)][:, :],
                                                           scalar=un_qkv, in1=kv_buf[:, c % 2, :], op0=ALU.mult,
                                                           op1=ALU.mult).then_inc(kv_done, 1)
                            dve.wait_ge(kv_done, g + 1)
                            dve.wait_ge(w_done, g + 1)
                            nc.vector.tensor_tensor(kv_buf[:, c % 2, :], kv_buf[:, c % 2, :], w_buf[:, c % 2, :],
                                                    ALU.mult).then_inc(wkv_done, 1)
                            dve.wait_ge(wkv_done, g + 1)
                            if not (isinstance(g, int) and g < KC):
                                dve.wait_ge(out_done, g - KC + 1)
                                dve.wait_ge(state_done, g - KC + 1)
                            nc.vector.tensor_tensor_scan(state[:, c, :], col(dec, c).to_broadcast([P, T]),
                                                         kv_buf[:, c % 2, :],
                                                         0.0 if t == 0 else state[:, c, T - 1:T], ALU.mult, ALU.add
                                                         ).then_inc(state_done, 1)
                            if wo and t == 0:
                                if c == KC - 1:
                                    for i in range(KC - 1):
                                        chunk_statistics(n, t, i)
                            elif c > 0:
                                chunk_statistics(n, t, c - 1)
                            if prep == "max" and t == 1 and c == 0:
                                for i in range(2):
                                    mod_peak(later_own[:, 2 + i:3 + i], 2 + i)
                                gates()
                            if prep == "max" and t < TPB - 1:
                                i = KC * t + c
                                dve.wait_ge(max_in[i % 2], 16 * (i // 2 + 1))
                                nc.vector.tensor_reduce(col(block_peaks, i), (stage_a, stage_b)[i % 2], AX.X, ALU.max,
                                                        apply_absolute_value=True).then_inc(block_peak, 1)
                            if c == 1:
                                h_next = h2t[0] if last and t == TPB - 1 else h1t[(t + 1) % 2]
                                for i in range(KC):
                                    dve.wait_ge(h1_read, KC * (n + 1) + i + 1)
                                    split(h_next[:, i, :], h_tmp[:, i % 2, :], h1_hi, KC * (n + 1) + i + 1,
                                          h1_done)
                                if wo and t == 0:
                                    split_n(n)
                                if prep == "max" and t == 0:
                                    output_scale()
                                if prep == "max" and t == TPB - 1:
                                    ffn_scales()
                            if prep == "max" and t == 0 and c == 2:
                                weight_low(3)
                        chunk_statistics(n, t, KC - 1)
                        if t == TPB - 1:
                            dve.wait_ge(out_stat, KC * (n + 1))
                            dve.sem_inc(passed, 1)
                            nc.vector.bn_aggr(gn_mv, gn_stats).then_inc(gn_mv_done, 1)
                    if last and t == TPB - 1:
                        split_n(n + 1)
                    if wo:
                        for c in range(TC):
                            dve.wait_ge(wo_ready, TC * n + c + 1)
                            dve.wait_ge(x1_done, TC * n + c - 1)
                            dve.wait_ge(gate_a_in, 16)
                            nc.vector.scalar_tensor_tensor(
                                out=o_tmp[:, c % 2, :], in0=ps[bank_wo(c, t, qkv)][:, :], scalar=un_o,
                                in1=gate_row(gate_a, b - 1), op0=ALU.mult, op1=ALU.mult).then_inc(wo_read, 1)

            def gate_row(tile, b):
                return tile.rearrange("p b d -> p (b d)")[:, bass.ds(b * D, D)]

            phase1(0, True, False, "max")
            with dve.Fori(1, 3) as b:
                phase1(b, True, True, "w13")
            phase1(3, True, True, "w2", last=True)
            phase1(4, False, True, "none")

            dve.wait_ge(prep2_out, 32 * TPB)

            def phase2(s, i, more, b):
                for k in SLOTS:
                    if isinstance(k, str):
                        if more:
                            for c in ((0, 1) if k == "t0" else (2, 3)):
                                dve.wait_ge(h2_read, KC * (s + 1) + c + 1)
                                split(h2t[1 - i][:, c, :], h2_tmp[:, c % 2, :], h2_hi, KC * (s + 1) + c + 1, h2_done)
                        continue
                    g = s * HC + k
                    buf = hid32[:, k % 2, :]
                    dve.wait_ge(sig_done, g + 1)
                    nc.vector.scalar_tensor_tensor(out=buf, in0=ps[bank_ffn(k)][:, :], scalar=un_gate, in1=buf,
                                                   op0=ALU.mult, op1=ALU.mult).then_inc(gated, 1)
                    dve.wait_ge(up_ready, g + 1)
                    dve.wait_ge(gated, g + HC + 1)
                    nc.vector.scalar_tensor_tensor(out=buf, in0=ps[bank_ffn(k) + 1][:, :], scalar=un_up, in1=buf,
                                                   op0=ALU.mult, op1=ALU.mult).then_inc(hid_done, 1)
                    if k == 4 and more:
                        dve.wait_ge(x1_in[1 - i], x1_count(s, i))
                        ln_statistics(x1[1 - i], ln2_stat, ln2_var, s + 1)
                    if k == 6 and more:
                        dve.wait_ge(ln2_rstd, s + 2)
                        normalise(xh, x1[1 - i], ln2_done)
                    dve.wait_ge(hid_hi, g + 1)
                    nc.vector.tensor_tensor(hid16[:, k % 2, T:2 * T], buf, hid16[:, k % 2, 0:T], ALU.subtract
                                            ).then_inc(hid_split, 1)
                for c in range(TC):
                    dve.wait_ge(acc_ready, TC * (s + 1) + c + 1)
                    dve.wait_ge(y_done, TC * (s + 1) + c - 1)
                    dve.wait_ge(gate_b_in, 16)
                    nc.vector.scalar_tensor_tensor(out=f_tmp[:, c % 2, :], in0=ps[c][:, :], scalar=un_w2,
                                                   in1=gate_row(gate_b, b), op0=ALU.mult, op1=ALU.mult
                                                   ).then_inc(acc_read, 1)

            def x1_count(s, i):
                return (s - i) * 8 + (16 if i == 0 else 32)

            with dve.Fori(0, NT // 2 - 1) as pair:
                phase2(pair * 2, 0, True, pair * 2 // TPB)
                phase2(pair * 2 + 1, 1, True, pair * 2 // TPB)
            phase2(NT - 2, 0, True, NB - 1)
            phase2(NT - 1, 1, False, NB - 1)

        @block.tensor
        def _(pe):
            def product(psum, pairs):
                for i, (a_hi, a_lo, b_hi, b_lo) in enumerate(pairs):
                    nc.tensor.matmul(psum, a_hi, b_hi, start=(i == 0), stop=False)
                    nc.tensor.matmul(psum, a_hi, b_lo, start=False, stop=False)
                    last = nc.tensor.matmul(psum, a_lo, b_hi, start=False, stop=(i == len(pairs) - 1))
                return last

            def transposes(dst_bank, src, c):
                for i in range(TC):
                    last = nc.tensor.transpose(ps[dst_bank][:, P * i:P * (i + 1)], src[:, i, P * c:P * (c + 1)], ident)
                return last

            def mod_rows_of(vectors, columns, done_in):
                for i, v in enumerate(vectors):
                    pe.wait_ge(done_in[i], 16)
                    for k in range(KC):
                        last = nc.tensor.matmul(ps[bank_mod(v)][0:NB, :], silu_c[:, NB * k:NB * (k + 1)],
                                                columns[:, k, D * i:D * (i + 1)], start=(k == 0), stop=(k == KC - 1))
                    last.then_inc(mod_ready, 1)

            def mod_channels(vectors):
                for i in vectors:
                    v = (SA, CA, SB, CB)[i]
                    pe.wait_ge(mod_copied, v + 1)
                    for c in range(KC):
                        last = nc.tensor.transpose(ps[bank_mod_t(i)][:, NB * c:NB * (c + 1)],
                                                   mod_rows[0:NB, v * D + P * c:v * D + P * (c + 1)], ident[0:NB, 0:NB])
                    last.then_inc(modt_ready, 1)

            pe.wait_ge(silu_done, 3)
            mod_rows_of((SA, CA), wmod_first, [wmod_in[0], wmod_in[0]])
            pe.wait_ge(ident_in, 16)
            mod_channels((0, 1))
            pe.wait_ge(ln_done, TC)
            for c in range(KC):
                transposes(c, xa, c).then_inc(t1_ready, 1)

            def hadamard_slice(t):
                pe.wait_ge(had_in, 16)
                pe.wait_ge(butterfly, 8 * (t + 1))
                for i in range(4):
                    nc.tensor.matmul(ps[i][:, :], had, stage_a[:, T * i:T * (i + 1)], start=True, stop=True
                                     ).then_inc(had_ready, 1)

            def phase1(b, qkv, wo, prep):
                for t in range(TPB):
                    n = b * TPB + t
                    if qkv:
                        h = h1t[t % 2]
                        pe.wait_ge(h1_done, KC * (n + 1))
                        for c in range(KC):
                            g = KC * n + c
                            for o, (matrix, ready) in enumerate(((0, v_ready), (1, k_ready), (2, r_ready))):
                                if o == 0 and not (isinstance(g, int) and g < 2):
                                    pe.wait_ge(r_read, g - 1)
                                if o == 1 and not (isinstance(g, int) and g < 1):
                                    pe.wait_ge(v_read, g)
                                if o == 2 and not (isinstance(g, int) and g < 1):
                                    pe.wait_ge(kv_done, g)
                                if isinstance(n, int) and n == 0 and c == 0:
                                    pe.wait_ge(wsplit, o + 1)
                                product(ps[bank_rkv(c, o)][:, :],
                                        [(w_rkv[:, KC * matrix + k, P * c:P * (c + 1)],
                                          w_rkv[:, KC * matrix + k, D + P * c:D + P * (c + 1)],
                                          h[:, k, 0:T], h[:, k, T:2 * T]) for k in range(KC)]).then_inc(ready, 1)
                            if c == 0 and prep == "w2" and t > 0:
                                pe.wait_ge(wo_read, TC * n)
                                hadamard_slice(t - 1)
                            if c == 0 and prep == "max" and t == 1:
                                mod_channels((2, 3))
                            if c == 1:
                                pe.wait_ge(ln_done, TC * (n + 2))
                                if wo:
                                    pe.wait_ge(wo_read, TC * n)
                                if prep == "w2" and t > 0:
                                    pe.wait_ge(had_read, 4 * t)
                                if prep == "max" and t == 0:
                                    pe.wait_ge(h1_read, KC)
                                if prep == "max" and t == 1:
                                    pe.wait_ge(wsplit, 4)
                                    pe.wait_ge(modt_copied, 4)
                                    pe.wait_ge(mod_copied, 6)
                                for i in range(KC):
                                    transposes(i, xa, i).then_inc(t1_ready, 1)
                        if prep == "max" and t == 0:
                            pe.wait_ge(h1_read, KC * 2)
                            mod_rows_of((GA, SB, CB, GB), wmod_rest, [wmod_in[1], wmod_in[1], wmod_in[2], wmod_in[2]])
                    if prep == "none" and t == 1:
                        pe.wait_ge(wo_read, TC * (n - 1))
                        hadamard_slice(TPB - 1)
                    if wo:
                        if qkv:
                            pe.wait_ge(h1_read, KC * (n + 2))
                        for k in range(KC):
                            pe.wait_ge(n_done, KC * n + k + 1)
                            for c in range(TC):
                                bank = bank_wo(c, t, qkv)
                                if k == 0 and (qkv or t >= 2):
                                    pe.wait_ge(wo_read, TC * (n - (1 if qkv else 2)) + c + 1)
                                if k == 0 and not qkv and t == 0:
                                    pe.wait_ge(kv_done, KC * NT)
                                    pe.wait_ge(r_read, KC * NT)
                                if k == 0 and not qkv and t == 1:
                                    pe.wait_ge(had_read, 4 * (TPB - 1) + c + 1)
                                hi, lo = n_t[:, k, P * c:P * (c + 1)], n_t[:, k, T + P * c:T + P * (c + 1)]
                                w_hi, w_lo = w_o[:, k, 0:D], w_o[:, k, D:2 * D]
                                nc.tensor.matmul(ps[bank][:, :], hi, w_hi, start=(k == 0), stop=False)
                                nc.tensor.matmul(ps[bank][:, :], hi, w_lo, start=False, stop=False)
                                last = nc.tensor.matmul(ps[bank][:, :], lo, w_hi, start=False, stop=(k == KC - 1))
                                if k == KC - 1:
                                    last.then_inc(wo_ready, 1)
                            if k < KC - 1:
                                last.then_inc(n_used, 1)

            phase1(0, True, False, "max")
            with pe.Fori(1, 3) as b:
                phase1(b, True, True, "w13")
            phase1(3, True, True, "w2")
            phase1(4, False, True, "none")

            pe.wait_ge(h1_done, KC * (NT + 1))
            pe.wait_ge(wo_read, TC * (NT + TPB - 1))

            def phase2(s, i, more):
                h = h2t[i]

                def down(k):
                    g = s * HC + k
                    if k % (HC // KC) == 0:
                        pe.wait_ge(w2_in[k // (HC // KC)], 16)
                    if k == 0:
                        pe.wait_ge(wo_read, TC * (NT + TPB))
                    pe.wait_ge(hid_hi, g + 1)
                    pe.wait_ge(hid_split, g + HC + 1)
                    for c in range(TC):
                        if k == 0:
                            pe.wait_ge(acc_read, TC * s + c + 1)
                        hi, lo = hid16[:, k % 2, P * c:P * (c + 1)], hid16[:, k % 2, T + P * c:T + P * (c + 1)]
                        w_hi, w_lo = w2_sb[:, k, 0:D], w2_sb[:, k, D:2 * D]
                        nc.tensor.matmul(ps[c][:, :], hi, w_hi, start=(k == 0), stop=False)
                        nc.tensor.matmul(ps[c][:, :], hi, w_lo, start=False, stop=False)
                        last = nc.tensor.matmul(ps[c][:, :], lo, w_hi, start=False, stop=(k == HC - 1))
                        if k == HC - 1:
                            last.then_inc(acc_ready, 1)
                    if k < HC - 1:
                        last.then_inc(w2_used, 1)

                before = None
                for j, k in enumerate(SLOTS):
                    bank = bank_ffn(k)
                    prior = SLOTS[j - 2]
                    if isinstance(prior, str) and more:
                        pe.wait_ge(h2_read, KC * (s + 1) + (2 if prior == "t0" else 4))
                    elif isinstance(prior, int):
                        pe.wait_ge(hid_done, s * HC + (prior + 1 if j < 2 else HC + prior + 1))
                    else:
                        pe.wait_ge(hid_done, s * HC + HC + SLOTS[j - 4] + 1)
                    if isinstance(k, str):
                        if more:
                            if k == "t0":
                                pe.wait_ge(ln2_done, TC * (s + 2))
                            for pair, c in enumerate((0, 1) if k == "t0" else (2, 3)):
                                transposes(bank + pair, xh, c).then_inc(t2_ready, 1)
                        continue
                    if k == 0:
                        pe.wait_ge(h2_done, KC * (s + 1))
                    if k % (HC // KC) == 0:
                        pe.wait_ge(w13_in[k // (HC // KC)], 16)
                    for matrix, ready in ((0, gate_ready), (1, up_ready)):
                        product(ps[bank + matrix][:, :],
                                [(w13_chunk(matrix, c, 0, k), w13_chunk(matrix, c, 1, k), h[:, c, 0:T],
                                  h[:, c, T:2 * T]) for c in range(KC)]).then_inc(ready, 1)
                    if before is not None:
                        down(before)
                    before = k
                down(before)

            with pe.Fori(0, NT // 2 - 1) as pair:
                phase2(pair * 2, 0, True)
                phase2(pair * 2 + 1, 1, True)
            phase2(NT - 2, 0, True)
            phase2(NT - 1, 1, False)


def kernel(L0_attn_x, L0_attn_Wr, L0_attn_Wk, L0_attn_Wv, L0_attn_Wo, L0_attn_decay, L0_attn_gn_weight, L0_attn_gn_bias,
           L0_ffn_W1, L0_ffn_W2, L0_ffn_W3, L0_c, L0_wmod):
    import concourse.bacc as bacc
    from concourse.bass_utils import run_bass_kernel_spmd

    def a(v):
        return np.asarray(v)

    def column(v):
        return a(v).reshape(KC, P).T

    had = np.ones((1, 1), np.float32)
    while had.shape[0] < P:
        had = np.block([[had, had], [had, -had]])
    arrays = {
        "x": a(L0_attn_x).reshape(NB * SEQ, D),
        "w_att": np.stack([a(L0_attn_Wv).T, a(L0_attn_Wk).T, a(L0_attn_Wr).T, a(L0_attn_Wo).T]),
        "w13": np.stack([a(L0_ffn_W1).T, a(L0_ffn_W3).T]),
        "w2t": a(L0_ffn_W2).T,
        "c_t": a(L0_c).T.reshape(KC, P, NB).transpose(1, 0, 2).reshape(P, KC * NB),
        "w_mod": a(L0_wmod),
        "columns": np.concatenate([column(L0_attn_decay), column(L0_attn_gn_weight), column(L0_attn_gn_bias)], axis=1),
        "identity": np.eye(P, dtype=np.float32),
        "hadamard": had,
    }
    arrays = {k: np.ascontiguousarray(v) for k, v in arrays.items()}
    nc = bacc.Bacc("TRN2", target_bir_lowering=False, num_devices=1)
    args = [nc.dram_tensor(k, v.shape, F32, kind="ExternalInput").ap() for k, v in arrays.items()]
    args.append(nc.dram_tensor("out", [NB * SEQ, D], F32, kind="ExternalOutput").ap())
    adaln_block_kernel(nc, *args)
    result = run_bass_kernel_spmd(nc, [arrays], core_ids=[0])
    return result.results[0]["out"].reshape(NB, SEQ, D)
```
